# Optimizing a Trainium2 kernel written in Bass

```python
import numpy as np
import jax
import jax.numpy as jnp

def _softmax(x, axis=-1):
    return jax.nn.softmax(x, axis=axis)

def _gelu(x):
    return jax.nn.gelu(x, approximate=True)

def _silu(x):
    return jax.nn.silu(x)

def _sigmoid(x):
    return jax.nn.sigmoid(x)

def _layernorm(x, axis=-1, eps=1e-05):
    m = jnp.mean(x, axis=axis, keepdims=True)
    v = jnp.var(x, axis=axis, keepdims=True)
    return (x - m) / jnp.sqrt(v + eps)

def _scatter_add(tgt, idx, src, axis=0):
    return tgt.at[idx].add(src)

def _segment_sum(src, seg, n):
    return jax.ops.segment_sum(src, seg, n)
kernel_name = 'mk_seq_preln_d1_jaxref_r8_d4a0fb'

def setup_inputs(seed: int=0):
    np.random.seed(seed)
    _w = jnp.asarray

    def _L0_attn_setup():
        import jax, jax.numpy as jnp
        import numpy as np
        B, T, HID = (4, 256, 128)
        H, D, V = (8, 64, 128)
        EPS = 1e-05

        def _rotary(x, T, D):
            inv_freq = 1.0 / 10000.0 ** (jnp.arange(0, D, 2, dtype=jnp.float32) / D)
            t = jnp.arange(T, dtype=jnp.float32)
            freqs = t[:, None] * inv_freq[None, :]
            emb = jnp.concatenate([freqs, freqs], axis=-1)
            cos = jnp.cos(emb)[None, None, :, :]
            sin = jnp.sin(emb)[None, None, :, :]
            x1, x2 = jnp.split(x, 2, axis=-1)
            rot = jnp.concatenate([-x2, x1], axis=-1)
            return x * cos + rot * sin
        key = jax.random.key(seed)
        ks = jax.random.split(key, 7)
        sc = 0.02
        return {'x': jax.random.normal(ks[0], (B, T, HID), dtype=jnp.float32), 'Wq': jax.random.normal(ks[1], (H * D, HID), dtype=jnp.float32) * sc, 'Wk': jax.random.normal(ks[2], (H * D, HID), dtype=jnp.float32) * sc, 'Wv': jax.random.normal(ks[3], (H * V, HID), dtype=jnp.float32) * sc, 'Wg': jax.random.normal(ks[4], (H * V, HID), dtype=jnp.float32) * sc, 'Wo': jax.random.normal(ks[5], (HID, H * V), dtype=jnp.float32) * sc, 'gn_weight': jnp.ones((H * V,), dtype=jnp.float32), 'gn_bias': jnp.zeros((H * V,), dtype=jnp.float32)}
    _L0_attn_in = _L0_attn_setup()

    def _L0_ffn_setup():
        import jax, jax.numpy as jnp
        import numpy as np
        E = 8
        D = 128
        F = 512
        S, B = (256, 2)
        LN_EPS = 1e-05

        def _moe_forward(input_features, centroids, ln_g, ln_b, W1, b1, W2, b2):
            s, b, d = input_features.shape
            x = jnp.swapaxes(input_features, 0, 1).reshape(-1, d)
            logits = x.astype(jnp.float32) @ centroids.astype(jnp.float32).T
            assign = jnp.argmax(logits, axis=-1)
            onehot = jax.nn.one_hot(assign, E, dtype=x.dtype)
            disp = jnp.einsum('te,td->etd', onehot, x)
            mu = disp.mean(-1, keepdims=True)
            var = disp.var(-1, keepdims=True)
            xn = (disp - mu) * jax.lax.rsqrt(var + LN_EPS)
            xn = xn * ln_g[:, None, :] + ln_b[:, None, :]
            h = jax.nn.relu(jnp.einsum('etd,edf->etf', xn, W1) + b1[:, None, :])
            y = jnp.einsum('etf,efd->etd', h, W2) + b2[:, None, :]
            y = disp + y
            out = jnp.einsum('te,etd->td', onehot, y)
            return jnp.swapaxes(out.reshape(b, s, d), 0, 1)
        key = jax.random.key(seed)
        ks = jax.random.split(key, 8)
        scale_in = 1.0 / np.sqrt(D)
        scale_ff = 1.0 / np.sqrt(F)
        return {'input_features': jax.random.normal(ks[0], (S, B, D), dtype=jnp.float32), 'centroids': jax.random.normal(ks[1], (E, D), dtype=jnp.float32) * scale_in, 'ln_g': jnp.ones((E, D), dtype=jnp.float32), 'ln_b': jnp.zeros((E, D), dtype=jnp.float32), 'W1': jax.random.normal(ks[2], (E, D, F), dtype=jnp.float32) * scale_in, 'b1': jax.random.normal(ks[3], (E, F), dtype=jnp.float32) * 0.01, 'W2': jax.random.normal(ks[4], (E, F, D), dtype=jnp.float32) * scale_ff, 'b2': jax.random.normal(ks[5], (E, D), dtype=jnp.float32) * 0.01}
    _L0_ffn_in = _L0_ffn_setup()
    _d = {'L0_attn_x': _L0_attn_in['x'], 'L0_attn_Wq': _L0_attn_in['Wq'], 'L0_attn_Wk': _L0_attn_in['Wk'], 'L0_attn_Wv': _L0_attn_in['Wv'], 'L0_attn_Wg': _L0_attn_in['Wg'], 'L0_attn_Wo': _L0_attn_in['Wo'], 'L0_attn_gn_weight': _L0_attn_in['gn_weight'], 'L0_attn_gn_bias': _L0_attn_in['gn_bias'], 'L0_ffn_centroids': _L0_ffn_in['centroids'], 'L0_ffn_ln_g': _L0_ffn_in['ln_g'], 'L0_ffn_ln_b': _L0_ffn_in['ln_b'], 'L0_ffn_W1': _L0_ffn_in['W1'], 'L0_ffn_b1': _L0_ffn_in['b1'], 'L0_ffn_W2': _L0_ffn_in['W2'], 'L0_ffn_b2': _L0_ffn_in['b2']}
    _x0 = _d['L0_attn_x']
    _d['L0_attn_x'] = jax.random.normal(jax.random.fold_in(jax.random.key(seed), 1), (2, 1024, 128), dtype=_x0.dtype)
    del _x0
    return _d

def reference(L0_attn_x, L0_attn_Wq, L0_attn_Wk, L0_attn_Wv, L0_attn_Wg, L0_attn_Wo, L0_attn_gn_weight, L0_attn_gn_bias, L0_ffn_centroids, L0_ffn_ln_g, L0_ffn_ln_b, L0_ffn_W1, L0_ffn_b1, L0_ffn_W2, L0_ffn_b2):

    def _L0_attn_ref(x, Wq, Wk, Wv, Wg, Wo, gn_weight, gn_bias):
        import jax, jax.numpy as jnp
        import numpy as np
        B, T, HID = (4, 256, 128)
        H, D, V = (8, 64, 128)
        EPS = 1e-05

        def _rotary(x, T, D):
            inv_freq = 1.0 / 10000.0 ** (jnp.arange(0, D, 2, dtype=jnp.float32) / D)
            t = jnp.arange(T, dtype=jnp.float32)
            freqs = t[:, None] * inv_freq[None, :]
            emb = jnp.concatenate([freqs, freqs], axis=-1)
            cos = jnp.cos(emb)[None, None, :, :]
            sin = jnp.sin(emb)[None, None, :, :]
            x1, x2 = jnp.split(x, 2, axis=-1)
            rot = jnp.concatenate([-x2, x1], axis=-1)
            return x * cos + rot * sin
        Bx, Tx, _ = x.shape
        q = jnp.einsum('bti,oi->bto', x, Wq).reshape(Bx, Tx, H, D).transpose(0, 2, 1, 3)
        k = jnp.einsum('bti,oi->bto', x, Wk).reshape(Bx, Tx, H, D).transpose(0, 2, 1, 3)
        v = jnp.einsum('bti,oi->bto', x, Wv).reshape(Bx, Tx, H, V).transpose(0, 2, 1, 3)
        g = jnp.einsum('bti,oi->bto', x, Wg)
        q = _rotary(q, Tx, D)
        k = _rotary(k, Tx, D)
        gamma = 1.0 - jnp.exp2(-5.0 - jnp.arange(H, dtype=jnp.float32))
        s = jnp.log2(gamma)
        n = jnp.arange(Tx, dtype=jnp.float32)
        rel = n[:, None] - n[None, :]
        causal = rel >= 0
        decay = jnp.where(causal[None, :, :], jnp.exp2(rel[None, :, :] * s[:, None, None]), 0.0)
        scores = jnp.einsum('bhtd,bhsd->bhts', q, k) * D ** (-0.5)
        scores = scores * decay[None]
        o = jnp.einsum('bhts,bhsv->bhtv', scores, v)
        o = o.transpose(0, 2, 1, 3)
        mean = jnp.mean(o, axis=-1, keepdims=True)
        var = jnp.var(o, axis=-1, keepdims=True)
        o = (o - mean) * jax.lax.rsqrt(var + EPS)
        o = o * gn_weight.reshape(H, V) + gn_bias.reshape(H, V)
        o = o.reshape(Bx, Tx, H * V)
        o = o * jax.nn.silu(g)
        return jnp.einsum('btc,oc->bto', o, Wo)

    def _L0_ffn_ref(input_features, centroids, ln_g, ln_b, W1, b1, W2, b2):
        import jax, jax.numpy as jnp
        import numpy as np
        E = 8
        D = 128
        F = 512
        S, B = (256, 2)
        LN_EPS = 1e-05

        def _moe_forward(input_features, centroids, ln_g, ln_b, W1, b1, W2, b2):
            s, b, d = input_features.shape
            x = jnp.swapaxes(input_features, 0, 1).reshape(-1, d)
            logits = x.astype(jnp.float32) @ centroids.astype(jnp.float32).T
            assign = jnp.argmax(logits, axis=-1)
            onehot = jax.nn.one_hot(assign, E, dtype=x.dtype)
            disp = jnp.einsum('te,td->etd', onehot, x)
            mu = disp.mean(-1, keepdims=True)
            var = disp.var(-1, keepdims=True)
            xn = (disp - mu) * jax.lax.rsqrt(var + LN_EPS)
            xn = xn * ln_g[:, None, :] + ln_b[:, None, :]
            h = jax.nn.relu(jnp.einsum('etd,edf->etf', xn, W1) + b1[:, None, :])
            y = jnp.einsum('etf,efd->etd', h, W2) + b2[:, None, :]
            y = disp + y
            out = jnp.einsum('te,etd->td', onehot, y)
            return jnp.swapaxes(out.reshape(b, s, d), 0, 1)
        return _moe_forward(input_features, centroids, ln_g, ln_b, W1, b1, W2, b2)
    x = L0_attn_x
    x = x + _L0_attn_ref(_layernorm(x, axis=-1), L0_attn_Wq, L0_attn_Wk, L0_attn_Wv, L0_attn_Wg, L0_attn_Wo, L0_attn_gn_weight, L0_attn_gn_bias)
    x = x + _L0_ffn_ref(_layernorm(x, axis=-1), L0_ffn_centroids, L0_ffn_ln_g, L0_ffn_ln_b, L0_ffn_W1, L0_ffn_b1, L0_ffn_W2, L0_ffn_b2)
    return x

_drawn_inputs = setup_inputs


def setup_inputs(seed=0):
    import zlib

    import numpy as np

    out = dict(_drawn_inputs(seed))
    spreads = {'L0_attn_gn_weight': (1.0, 0.2),
     'L0_attn_gn_bias': (0.0, 0.1),
     'L0_ffn_ln_g': (1.0, 0.2),
     'L0_ffn_ln_b': (0.0, 0.1)}
    factors = {'L0_ffn_b1': 8.0, 'L0_ffn_b2': 8.0}
    for name, (base, spread) in spreads.items():
        noise = np.random.default_rng([zlib.crc32(name.encode()), seed]).standard_normal(out[name].shape)
        drawn = base * np.exp(spread * noise) if base else spread * noise
        out[name] = jnp.asarray(drawn.astype(out[name].dtype))
    for name, factor in factors.items():
        out[name] = (out[name] * factor).astype(out[name].dtype)
    return out
```

```python
from contextlib import ExitStack

import numpy as np

import concourse.bass as bass
from concourse import mybir

F32 = mybir.dt.float32
F32R = mybir.dt.float32r
I32 = mybir.dt.int32
U32 = mybir.dt.uint32
ALU = mybir.AluOpType
ACT = mybir.ActivationFunctionType
AX = mybir.AxisListType
ds = bass.ds

P = 128
B, T, HID = 2, 1024, 128
H, D, V = 8, 64, 128
NC = T // P
HP = H // 2
E, F = 8, 512
FC = F // P
EPS = 1e-5
NTOK = B * T
NT = NTOK // P
SLOTS = NT + E - 1
SLOTW = 24
RING = 4
PAD_ROW = 4096

_at = 0


def _col(n):
    global _at
    _at += n
    return slice(_at - n, _at)


C_ID = _col(P)
C_COS = _col(NC * D)
C_SIN = _col(NC * D)
C_GV = _col(H)
C_EPS = _col(H)
C_GC = _col(HP)
C_MISC0 = _col(0)
C_MASK = _col(H * P)
C_TRI = _col(P)
C_IOTA = _col(P)
C_SLOT = _col(SLOTW)
C_FIRST = _col(E)
C_STEP = _col(NT)
C_TOK = _col(NT)
C_ALL = _at


def constants():
    c = np.zeros((P, C_ALL), np.float32)
    i = np.arange(P)
    c[:, C_ID] = np.eye(P)
    inv = (np.float32(1.0) / np.float32(10000.0) ** (np.arange(0, D, 2, dtype=np.float32) / np.float32(D))).astype(np.float32)
    ang = np.arange(T, dtype=np.float32)[:, None] * inv[None, :]
    cos = np.concatenate([np.cos(ang), np.cos(ang)], 1)
    sin = np.concatenate([-np.sin(ang), np.sin(ang)], 1)
    c[:, C_COS] = cos.reshape(NC, P, D).transpose(1, 0, 2).reshape(P, -1)
    c[:, C_SIN] = sin.reshape(NC, P, D).transpose(1, 0, 2).reshape(P, -1)
    gamma = 1.0 - 2.0 ** (-5.0 - np.arange(H, dtype=np.float64))
    c[:, C_GV] = gamma[None, :] ** (P - i)[:, None]
    c[:, C_EPS] = D * EPS * gamma[None, :] ** (-2.0 * i)[:, None]
    for half in range(2):
        c[half * D:(half + 1) * D, C_GC] = gamma[half::2] ** P
    causal = (i[None, :] >= i[:, None]).astype(np.float64)
    order = [2 * p + half for half in range(2) for p in range(HP)]
    c[:, C_MASK] = (causal[:, None, :] * gamma[order][None, :, None] ** -P).reshape(P, -1)
    c[:, C_TRI] = i[:, None] < i[None, :]
    c[:, C_IOTA] = i
    c[:, C_SLOT] = np.arange(SLOTW)
    c[:, C_FIRST] = E - np.arange(E)
    c[:, C_STEP] = P * np.arange(NT)
    tok = (np.arange(B)[None, None, :] * T + np.arange(NC)[None, :, None] * P + i[:, None, None]) + 1
    c[:, C_TOK] = tok.reshape(P, NT)
    return c


def preln_retention_moe_kernel(nc, x_in, wqkvg_in, wo_in, gn_in, cen_in, lng_in, lnb_in,
                               w1_in, b1_in, w2_in, b2_in, const_in, out):
    ctx = ExitStack()
    with ctx:
        def sb(name, shape, dt=F32):
            return ctx.enter_context(nc.sbuf_tensor(name, shape, dt))

        def sem(name):
            return ctx.enter_context(nc.semaphore(name))

        payload = nc.dram_tensor("payload", (NTOK, 2 * HID), F32, kind="Internal").ap()

        cst = sb("cst", [P, C_ALL])
        x_all = sb("x_all", [P, B, NC, HID])
        w_raw = sb("w_raw", [P, E * F])
        w_hi = sb("w_hi", [P, 3072], F32R)
        w_lo = sb("w_lo", [P, 3072], F32R)
        wo = sb("wo", [P, H, HID])
        gn = sb("gn", [P, 2, H])
        cen = sb("cen", [P, E])
        lng = sb("lng", [P, E])
        lnb = sb("lnb", [P, E])
        w1_stage = sb("w1_stage", [P, F])
        w1_hi = sb("w1_hi", [P, E * F], F32R)
        w1_lo = sb("w1_lo", [P, E * F], F32R)
        w2 = sb("w2", [P, E, FC, HID])
        b2_rep = sb("b2_rep", [P, E * HID])
        b1_rep = w_raw

        xn = sb("xn", [P, B, HID])
        xT_hi = sb("xT_hi", [P, B, P], F32R)
        xT_lo = sb("xT_lo", [P, B, P], F32R)
        rot = sb("rot", [P, 4, 512])
        rot_sin = sb("rot_sin", [P, 2, 512])
        vg = sb("vg", [P, B, H * V])
        qkT = sb("qkT", [P, 4, 512])
        prob = sb("prob", [P, B, 2, 512])
        state = sb("state", [P, B, HP * V])
        z = sb("z", [P, B, H * V])
        sg = sb("sg", [P, 2, H, B * P])
        za = sb("za", [P, H, B * P])
        yT = sb("yT", [P, H, B * P])
        x2 = sb("x2", [P, B, HID])
        z2 = sb("z2", [P, B, HID])
        z2T = sb("z2T", [P, B, P])
        rows = sb("rows", [P, B, 2 * HID])
        logit = sb("logit", [P, NC, B, E])
        half_row = sb("half_row", [P, H])
        small = sb("small", [P, 256])

        st_x = small[:, 0:12].rearrange("p (g s) -> p g s", g=B)
        mean_x = small[:, 12:14]
        eps_row = small[:, 208:210]
        ve_x, rs_x = small[:, 16:18], small[:, 18:20]
        st_z = small[:, 20:32].rearrange("p (g s) -> p g s", g=B)
        mean_z = small[:, 32:34]
        ve_z, rs_z = small[:, 36:38], small[:, 38:40]
        st_u = small[:, 40:136].rearrange("p (b h s) -> p b h s", b=B, h=H)
        ve_u = small[:, 136:152].rearrange("p (b h) -> p b h", b=B)
        rs_u = small[:, 152:168].rearrange("p (b h) -> p b h", b=B)
        mean_u = small[:, 168:184].rearrange("p (b h) -> p b h", b=B)
        tmp_u = small[:, 184:208].rearrange("p (k h) -> p k h", k=3)

        bankA, bankB, bankC, bankD = [ctx.enter_context(nc.psum_tensor(f"bank{c}", [P, 512], F32)) for c in "ABCD"]
        ring = [bankA, bankB, bankC, bankD]
        bankU = [[ctx.enter_context(nc.psum_tensor(f"bankU{b}{par}", [P, 512], F32)) for par in range(2)] for b in range(B)]

        zf = z[:, :, :].rearrange("p b n -> p (b n)")
        sgf = sg[:, :, :, :].rearrange("p a h n -> p (a h n)")
        one_row = zf[:, 0:2048].rearrange("p (t r) -> p t r", t=NT)
        one_slot = sgf[:, 0:NT * SLOTW].rearrange("p (t s) -> p t s", t=NT)
        rt = sgf[:, 512:4096]
        ones = za[:, 0, 0:P]
        mx = rt[:, 0:16]
        mw = rt[:, 16:32]
        eq = rt[:, 32:160].rearrange("p (t e) -> p t e", t=NT)
        oh = rt[:, 160:288].rearrange("p (t e) -> p t e", t=NT)
        scan0 = rt[:, 288:480].rearrange("p (t e) -> p t e", e=E)
        scan1 = rt[:, 480:672].rearrange("p (t e) -> p t e", e=E)
        over = rt[:, 672:800].rearrange("p (e j) -> p e j", e=E)
        ntile = rt[:, 800:808]
        tile_end = rt[:, 808:816]
        tile_start = rt[:, 816:824]
        zero8 = rt[:, 824:832]
        place = rt[:, 832:960].rearrange("p (t e) -> p t e", t=NT)
        pos = rt[:, 960:976]
        slot_f = rt[:, 976:992]
        row_f = rt[:, 992:1008]
        below = rt[0:1, 1008:1200].rearrange("p (k e) -> p k e", e=E)
        expert_f = rt[0:1, 1200:1224]
        empty = rt[:, 1224:1248]
        ids = rt[:, 1248:1272]
        idx = sb("idx", [P, 160], I32)
        pos_i, slot_i, row_i = idx[:, 0:16], idx[:, 16:32], idx[:, 32:48]
        gather_i = sb("gather_i", [P, SLOTW], U32)
        scatter_i = sb("scatter_i", [P, SLOTW], U32)
        gather_at = sb("gather_at", [P, RING], U32)
        scatter_at = sb("scatter_at", [P, RING], U32)
        expert_i = sb("expert_i", [1, SLOTW], I32)

        yf = yT[:, :, :].rearrange("p h n -> p (h n)")
        vf = vg[:, :, :].rearrange("p b n -> p (b n)")
        pf = prob[:, :, :, :].rearrange("p b a n -> p (b a n)")
        erow = yf[:, 0:RING * 256].rearrange("p (r n) -> p r n", r=RING)
        eout = yf[:, RING * 256:RING * 384].rearrange("p (r n) -> p r n", r=RING)
        resid = yf[:, 1536:1536 + P]
        exT = vf[:, 0:P]
        hid = vf[:, 512:1024]
        hidT = pf[:, 0:512].rearrange("p (c t) -> p c t", c=FC)
        ex_hi = sb("ex_hi", [P, P], F32R)
        ex_lo = sb("ex_lo", [P, P], F32R)

        ident = cst[:, C_ID]
        cos_t = cst[:, C_COS].rearrange("p (n d) -> p n d", d=D)
        sin_t = cst[:, C_SIN].rearrange("p (n d) -> p n d", d=D)
        mask_t = cst[:, C_MASK].rearrange("p (a n) -> p a n", a=2)

        x_in_sem = sem("x_in_sem")
        c_in = [sem(f"c_in{i}") for i in range(2)]
        w_in = [sem(f"w_in{i}") for i in range(3)]
        small_in = sem("small_in")
        wo_in_sem = sem("wo_in_sem")
        w1_in_sem = sem("w1_in_sem")
        w2_in_sem = sem("w2_in_sem")
        b_in = [sem("b1_in_sem"), sem("b2_in_sem")]
        w_hi_done, w_lo_done = sem("w_hi_done"), sem("w_lo_done")
        w1_hi_done, w1_lo_done = sem("w1_hi_done"), sem("w1_lo_done")
        x_var, x_rstd = sem("x_var"), sem("x_rstd")
        xn_done = sem("xn_done")
        xT_mm, xT_hi_done, xT_lo_done = sem("xT_mm"), sem("xT_hi_done"), sem("xT_lo_done")
        g_mm, sg_done = sem("g_mm"), sem("sg_done")
        qk_mm, rot_mul, rot_add = sem("qk_mm"), sem("rot_mul"), sem("rot_add")
        v_mm, v_done = sem("v_mm"), sem("v_done")
        qkT_mm, qkT_done = sem("qkT_mm"), sem("qkT_done")
        sc_mm, sc_done = sem("sc_mm"), sem("sc_done")
        u_mm, u_var, u_rstd, z_done = sem("u_mm"), sem("u_var"), sem("u_rstd"), sem("z_done")
        st_mm, st_done = sem("st_mm"), sem("st_done")
        zT_mm, za_done, y_done = sem("zT_mm"), sem("za_done"), sem("y_done")
        wo_mm, x2_done = sem("wo_mm"), sem("x2_done")
        z_var, z_rstd, z2_done, rn_done, rs_done = (sem(n) for n in ("z_var", "z_rstd", "z2_done", "rn_done", "rs_done"))
        z2T_mm, z2T_done, lg_mm, lg_done = sem("z2T_mm"), sem("z2T_done"), sem("lg_mm"), sem("lg_done")
        pay_out = sem("pay_out")
        dve = sem("dve_chain")
        ones_done, oh_done, rank_mm, one_done, ids_mm, ids_done = (
            sem(n) for n in ("ones_done", "oh_done", "rank_mm", "one_done", "ids_mm", "ids_done"))
        row_placed = sem("row_placed")
        e_in = [sem(f"e_in{i}") for i in range(RING)]
        e_out = [sem(f"e_out{i}") for i in range(RING)]
        ezT_mm, exT_done, ex_hi_done, ex_lo_done = (sem(n) for n in ("ezT_mm", "exT_done", "ex_hi_done", "ex_lo_done"))
        h_mm, h_done, hT_mm, hT_done = (sem(n) for n in ("h_mm", "h_done", "hT_mm", "hT_done"))
        y_mm, eo_done, resid_done = (sem(n) for n in ("y_mm", "eo_done", "resid_done"))

        block = ctx.enter_context(nc.Block())

        @block.sync
        def _(sp):
            sp.dma_start(x_all[:, :, :, :], x_in.rearrange("b (n p) d -> p b n d", p=P)).then_inc(x_in_sem, 16)
            sp.dma_start(cst[:, 0:C_MISC0.start], const_in[:, 0:C_MISC0.start]).then_inc(c_in[0], 16)
            for i in range(3):
                sp.dma_start(w_raw[:, 1024 * i:1024 * i + 1024], wqkvg_in[:, 1024 * i:1024 * i + 1024]).then_inc(w_in[i], 16)
            sp.dma_start(cst[:, C_MISC0.start:C_ALL], const_in[:, C_MISC0.start:C_ALL]).then_inc(c_in[1], 16)
            sp.dma_start(gn[:, :, :], gn_in).then_inc(small_in, 16)
            sp.dma_start(cen[:, :], cen_in).then_inc(small_in, 16)
            sp.dma_start(lng[:, :], lng_in).then_inc(small_in, 16)
            sp.dma_start(lnb[:, :], lnb_in).then_inc(small_in, 16)
            sp.dma_start(wo[:, :, :], wo_in).then_inc(wo_in_sem, 16)
            sp.dma_start(w1_stage[:, :], w1_in[:, 0, :]).then_inc(w1_in_sem, 16)
            sp.dma_start(w2[:, :, :, :], w2_in).then_inc(w2_in_sem, 16)
            sp.dma_start(b2_rep[:, :], b2_in.partition_broadcast(P)).then_inc(b_in[1], 16)
            sp.wait_ge(w_lo_done, 3)
            sp.dma_start(b1_rep[:, :], b1_in.partition_broadcast(P)).then_inc(b_in[0], 16)

            def step(n):
                sp.wait_ge(w1_lo_done, n)
                sp.dma_start(w1_stage[:, :], w1_in[:, ds(n, 1), :].rearrange("p a f -> p (a f)")).then_inc(w1_in_sem, 16)

            def store_rows(n):
                sp.wait_ge(rn_done, n)
                sp.wait_ge(rs_done, n)
                sp.dma_start(payload.rearrange("(b n p) c -> p b n c", b=B, p=P)[:, :, ds(n - 1, 1), :]
                             .rearrange("p b a c -> p b (a c)"), rows[:, :, :]).then_inc(pay_out, 16)

            with sp.Fori(1, NC) as n:
                step(n)
                store_rows(n)
            store_rows(NC)

        @block.gpsimd
        def _(pool):
            pool.memset(half_row[:, :], -0.5).then_inc(ones_done, 1)
            pool.memset(logit[:, :, :, :], 0.0).then_inc(lg_done, 1)
            pool.wait_ge(ones_done, 1)

            def rstd(out_ap, in_ap, done):
                pool.tensor_tensor(out_ap, in_ap, half_row[:, 0:in_ap.shape[1]], ALU.pow).then_inc(done, 1)

            def step(n, has_cur, has_prev, has_next):
                if has_cur:
                    for i in range(4):
                        pool.wait_ge(rot_mul, 4 * n + i + 1)
                        pool.tensor_tensor(rot[:, i, :], rot[:, i, :], rot_sin[:, i % 2, :], ALU.add).then_inc(rot_add, 1)
                if has_next:
                    pool.wait_ge(x_var, n + 2)
                    rstd(rs_x, ve_x, x_rstd)
                if has_prev:
                    for j in range(4):
                        pool.wait_ge(za_done, 4 * n - 4 + j + 1)
                        pool.wait_ge(sg_done, 4 * n - 4 + j + 1)
                        pool.tensor_tensor(yT[:, 2 * j:2 * j + 2, :].rearrange("p h n -> p (h n)"),
                                           za[:, 2 * j:2 * j + 2, :].rearrange("p h n -> p (h n)"),
                                           sg[:, ds((n - 1) % 2, 1), 2 * j:2 * j + 2, :].rearrange("p a h n -> p (a h n)"),
                                           ALU.mult).then_inc(y_done, 1)
                    pool.wait_ge(z_var, 2 * n - 1)
                    rstd(rs_z, ve_z, z_rstd)
                    pool.wait_ge(z2_done, n)
                    pool.tensor_tensor(rows[:, :, 0:HID], x2[:, :, :], z2[:, :, :], ALU.add).then_inc(rs_done, 1)
                    pool.wait_ge(z_var, 2 * n)
                    rstd(rs_z, ve_z, z_rstd)
                if has_cur:
                    for b in range(B):
                        pool.wait_ge(u_var, 2 * n + b + 1)
                        rstd(rs_u[:, b, :], ve_u[:, b, :], u_rstd)
                if has_prev:
                    pool.wait_ge(pay_out, 16 * n)

            pool.wait_ge(x_var, 1)
            rstd(rs_x, ve_x, x_rstd)
            step(0, True, False, True)
            with pool.Fori(1, NC - 1) as n:
                step(n, True, True, True)
            step(NC - 1, True, True, False)
            step(NC, False, True, False)

            pool.wait_ge(ids_done, 2)
            pool.wait_ge(pay_out, 16 * NC)

            last_token = pool.to_reg(NTOK - 1)

            def place_gather(k, j):
                return pool.tensor_copy(gather_at[:, j:j + 1], gather_i[:, ds(k, 1)])

            def place_scatter(k, j):
                return pool.tensor_copy(scatter_at[:, j:j + 1], scatter_i[:, ds(k, 1)])

            def gather(j):
                pool.indirect_dma_start(out=erow[:, j, :], out_offset=None, in_=payload,
                                        in_offset=bass.IndirectOffsetOnAxis(ap=gather_at[:, j:j + 1], axis=0),
                                        bounds_check=last_token, oob_is_err=False).then_inc(e_in[j], 16)

            def scatter(j):
                pool.indirect_dma_start(out=out.rearrange("b t d -> (b t) d"), in_=eout[:, j, :], in_offset=None,
                                        out_offset=bass.IndirectOffsetOnAxis(ap=scatter_at[:, j:j + 1], axis=0),
                                        bounds_check=last_token, oob_is_err=False).then_inc(e_out[j], 16)

            def tile(k, j, turn, has_gather, has_scatter):
                e = pool.value_load(expert_i[0:1, ds(k, 1)], min_val=0, max_val=E - 1)
                if has_gather:
                    place_gather(k + 2, (j + 2) % RING)
                place_scatter(k - 1 if has_scatter else SLOTS - 1, (j - 1) % RING).then_inc(row_placed, 1)
                pool.wait_ge(row_placed, k + 3)
                pool.wait_ge(e_in[j], 16 * (turn + 1))
                pool.wait_ge(eo_done, k)
                pool.tensor_tensor(resid, erow[:, j, 0:HID], b2_rep[:, ds(e * HID, HID)], ALU.add).then_inc(resid_done, 1)
                if has_gather:
                    gather((j + 2) % RING)
                if has_scatter:
                    scatter((j - 1) % RING)

            pool.wait_ge(b_in[1], 16)
            for j in range(2):
                place_gather(j, j).then_inc(row_placed, 1)
            pool.wait_ge(row_placed, 2)
            gather(0)
            gather(1)
            for j in range(RING):
                tile(j, j, 0, True, j > 0)
            with pool.Fori(1, (SLOTS - 3) // RING) as m:
                for j in range(RING):
                    tile(m * RING + j, j, m, True, True)
            for j in range(3):
                k = SLOTS - 3 + j
                tile(k, j, SLOTS // RING, j < 1, True)
            place_scatter(SLOTS - 1, (SLOTS - 1) % RING).then_inc(row_placed, 1)
            pool.wait_ge(row_placed, SLOTS + 3)
            pool.wait_ge(eo_done, SLOTS)
            scatter((SLOTS - 1) % RING)
            for j in range(RING):
                pool.wait_ge(e_out[j], 16 * len(range(j, SLOTS, RING)))

        @block.scalar
        def _(act):
            for i in range(3):
                act.wait_ge(w_in[i], 16)
                act.activation(w_hi[:, 1024 * i:1024 * i + 1024], w_raw[:, 1024 * i:1024 * i + 1024], ACT.Copy).then_inc(w_hi_done, 1)

            def x_high(n):
                act.wait_ge(xT_mm, n + 1)
                act.activation(xT_hi[:, :, :].rearrange("p b t -> p (b t)"), bankA[:, 0:B * P], ACT.Copy).then_inc(xT_hi_done, 1)

            def step(n, has_cur, has_prev, has_next):
                if has_cur:
                    for j in range(4):
                        act.wait_ge(g_mm, 4 * n + j + 1)
                        act.activation(sg[:, ds(n % 2, 1), 2 * j:2 * j + 2, :].rearrange("p a h n -> p (a h n)"),
                                       ring[j][:, :], ACT.Silu).then_inc(sg_done, 1)
                if has_prev:
                    for j in range(4):
                        act.wait_ge(zT_mm, 4 * n - 4 + j + 1)
                        for h in (2 * j, 2 * j + 1):
                            a = act.activation(za[:, h, :], ring[j][:, (h % 2) * 256:(h % 2) * 256 + 256], ACT.Identity,
                                               scale=gn[:, 0, h:h + 1], bias=gn[:, 1, h:h + 1])
                        a.then_inc(za_done, 1)
                if has_cur:
                    for i in range(4):
                        act.wait_ge(qkT_mm, 4 * n + i + 1)
                        act.activation(qkT[:, i, :], ring[i][:, :], ACT.Copy).then_inc(qkT_done, 1)
                if has_next:
                    x_high(n + 1)
                if has_cur:
                    act.wait_ge(w1_in_sem, 16 * n + 16)
                    act.activation(w1_hi[:, ds(n * F, F)], w1_stage[:, :], ACT.Copy).then_inc(w1_hi_done, 1)
                if has_prev:
                    act.wait_ge(z2T_mm, n)
                    act.activation(z2T[:, :, :].rearrange("p b t -> p (b t)"), bankA[:, 0:B * P], ACT.Copy).then_inc(z2T_done, 1)
                    act.wait_ge(lg_mm, n)
                    act.activation(logit[:, ds(n - 1, 1), :, :].rearrange("p a b e -> p (a b e)"), bankB[:, 0:B * E], ACT.Copy).then_inc(lg_done, 1)
                    act.wait_ge(y_done, 4 * n)

            x_high(0)
            act.wait_ge(small_in, 64)
            step(0, True, False, True)
            with act.Fori(1, NC - 1) as n:
                step(n, True, True, True)
            step(NC - 1, True, True, False)
            step(NC, False, True, False)

            def high(k):
                act.wait_ge(exT_done, k + 1)
                act.activation(ex_hi[:, :], exT, ACT.Copy).then_inc(ex_hi_done, 1)

            def tile(k, has_next):
                if has_next:
                    high(k + 1)
                act.wait_ge(hT_mm, k + 1)
                act.activation(hidT.rearrange("p c t -> p (c t)"), bankB[:, :], ACT.Relu).then_inc(hT_done, 1)

            high(0)
            tile(0, True)
            with act.Fori(1, SLOTS - 1) as k:
                tile(k, True)
            tile(SLOTS - 1, False)

        @block.tensor
        def _(pe):
            def split3(out_ap, l_hi, l_lo, r_hi, r_lo):
                pe.matmul(out_ap, l_hi, r_hi, start=True, stop=False)
                pe.matmul(out_ap, l_hi, r_lo, start=False, stop=False)
                return pe.matmul(out_ap, l_lo, r_hi, start=False, stop=True)

            def x_turn(n):
                pe.wait_ge(xn_done, n + 1)
                for b in range(B):
                    mm = pe.transpose(bankA[:, b * P:(b + 1) * P], xn[:, b, :], ident)
                mm.then_inc(xT_mm, 1)

            def project(n, has_prev):
                pe.wait_ge(xT_lo_done, n + 1)
                for j in range(4):
                    if has_prev and j == 0:
                        pe.wait_ge(sc_done, 4 * n)
                    if has_prev and j == 1:
                        pe.wait_ge(lg_done, n)
                    if has_prev and j >= 2:
                        pe.wait_ge(st_done, 2 * n - 3 + j)
                    for c in (2 * j, 2 * j + 1):
                        s = slice(c * P, (c + 1) * P)
                        mm = split3(ring[j][:, (c % 2) * 256:(c % 2) * 256 + 256], w_hi[:, s], w_lo[:, s],
                                    xT_hi[:, :, :].rearrange("p b t -> p (b t)"), xT_lo[:, :, :].rearrange("p b t -> p (b t)"))
                    mm.then_inc(g_mm, 1)
                if not has_prev:
                    pe.wait_ge(w_lo_done, 2)
                for i in range(4):
                    pe.wait_ge(sg_done, 4 * n + i + 1)
                    s = slice(1024 + 512 * (i % 2), 1536 + 512 * (i % 2))
                    split3(ring[i][:, :], xT_hi[:, i // 2, :], xT_lo[:, i // 2, :], w_hi[:, s], w_lo[:, s]).then_inc(qk_mm, 1)

            def project_v(n, has_prev):
                if not has_prev:
                    pe.wait_ge(w_lo_done, 3)
                for i in range(4):
                    if has_prev:
                        pe.wait_ge(za_done, 4 * n - 4 + i + 1)
                    else:
                        pe.wait_ge(rot_mul, 4 * n + i + 1)
                    s = slice(2048 + 512 * (i % 2), 2560 + 512 * (i % 2))
                    split3(ring[i][:, :], xT_hi[:, i // 2, :], xT_lo[:, i // 2, :], w_hi[:, s], w_lo[:, s]).then_inc(v_mm, 1)

            def turn_z(n, has_cur):
                pe.wait_ge(z_done, 2 * n)
                for j in range(4):
                    if has_cur:
                        pe.wait_ge(rot_mul, 4 * n + j + 1)
                    else:
                        pe.wait_ge(sc_done, 4 * n)
                        pe.wait_ge(lg_done, n)
                    for h in (2 * j, 2 * j + 1):
                        for b in range(B):
                            c = (h % 2) * 256 + b * P
                            mm = pe.transpose(ring[j][:, c:c + P], z[:, b, h * V:(h + 1) * V], ident)
                    mm.then_inc(zT_mm, 1)

            def turn_qk(n):
                for i in range(4):
                    pe.wait_ge(rot_add, 4 * n + i + 1)
                    pe.wait_ge(v_done, 4 * n + i + 1)
                    for p in range(HP):
                        mm = pe.transpose(ring[i][:, p * P:(p + 1) * P], rot[:, i, p * P:(p + 1) * P], ident)
                    mm.then_inc(qkT_mm, 1)

            SC = [[bankB, bankC], [bankD, bankA]]

            def scores(n, b, has_next):
                pe.wait_ge(qkT_done, 4 * n + 2 * b + 2)
                if b == 0:
                    pe.wait_ge(qkT_done, 4 * n + 3)
                else:
                    pe.wait_ge(qkT_done, 4 * n + 4)
                    if has_next:
                        pe.wait_ge(xT_lo_done, n + 2)
                for h in range(H):
                    par, p = h % 2, h // 2
                    q = qkT[par * D:(par + 1) * D, 2 * b, p * P:(p + 1) * P]
                    k = qkT[par * D:(par + 1) * D, 2 * b + 1, p * P:(p + 1) * P]
                    mm = pe.matmul(SC[b][par][:, p * P:(p + 1) * P], k, q, start=True, stop=True)
                    if h >= H - 2:
                        mm.then_inc(sc_mm, 1)

            def project_out(n, has_cur):
                pe.wait_ge(y_done, 4 * n)
                if has_cur:
                    pe.wait_ge(sc_done, 4 * n + 1)
                else:
                    pe.wait_ge(za_done, 4 * n)
                for b in range(B):
                    for h in range(H):
                        mm = pe.matmul(bankB[:, b * HID:(b + 1) * HID], yT[:, h, b * P:(b + 1) * P], wo[:, h, :],
                                       start=(h == 0), stop=(h == H - 1))
                mm.then_inc(wo_mm, 1)

            def retain(n, b, has_prev):
                pe.wait_ge(sc_done, 4 * n + 2 * b + 2)
                if has_prev:
                    pe.wait_ge(z_done, 2 * n - 2 + b + 1)
                    pe.wait_ge(st_done, 2 * n - 2 + b + 1)
                for p in range(HP):
                    if has_prev:
                        for par in range(2):
                            hs = slice(par * D, (par + 1) * D)
                            pe.matmul(bankU[b][par][:, p * V:(p + 1) * V], qkT[hs, 2 * b, p * P:(p + 1) * P],
                                      state[hs, b, p * V:(p + 1) * V], start=True, stop=False)
                    for par in range(2):
                        h = 2 * p + par
                        mm = pe.matmul(bankU[b][par][:, p * V:(p + 1) * V], prob[:, b, par, p * P:(p + 1) * P],
                                       vg[:, b, h * V:(h + 1) * V], start=not has_prev, stop=True)
                mm.then_inc(u_mm, 1)

            def update_state(n, b):
                for h in range(H):
                    par, p = h % 2, h // 2
                    mm = pe.matmul([bankC, bankD][b][par * D:(par + 1) * D, p * V:(p + 1) * V],
                                   rot[:, 2 * b + 1, h * D:(h + 1) * D], vg[:, b, h * V:(h + 1) * V], start=True, stop=True)
                mm.then_inc(st_mm, 1)

            def turn_z2(n, has_cur):
                pe.wait_ge(z2_done, n)
                if has_cur:
                    pe.wait_ge(sc_done, 4 * n + 4)
                for b in range(B):
                    mm = pe.transpose(bankA[:, b * P:(b + 1) * P], z2[:, b, :], ident)
                mm.then_inc(z2T_mm, 1)

            def logits(n):
                pe.wait_ge(z2T_done, n)
                pe.wait_ge(x2_done, n)
                for b in range(B):
                    mm = pe.matmul(bankB[:, b * E:(b + 1) * E], z2T[:, b, :], cen[:, :], start=True, stop=True)
                mm.then_inc(lg_mm, 1)

            def step(n, has_cur, has_prev, has_next):
                if has_cur:
                    project(n, has_prev)
                if has_prev:
                    turn_z(n, has_cur)
                if has_cur:
                    project_v(n, has_prev)
                    turn_qk(n)
                    if has_next:
                        pe.wait_ge(qkT_done, 4 * n + 1)
                        x_turn(n + 1)
                    scores(n, 0, has_next)
                    scores(n, 1, has_next)
                if has_prev:
                    project_out(n, has_cur)
                if has_cur:
                    retain(n, 0, has_prev)
                    retain(n, 1, has_prev)
                if has_prev:
                    turn_z2(n, has_cur)
                if has_next:
                    update_state(n, 0)
                    update_state(n, 1)
                if has_prev:
                    logits(n)

            pe.wait_ge(c_in[0], 16)
            x_turn(0)
            pe.wait_ge(w_lo_done, 1)
            step(0, True, False, True)
            pe.wait_ge(wo_in_sem, 16)
            with pe.Fori(1, NC - 1) as n:
                step(n, True, True, True)
            step(NC - 1, True, True, False)
            step(NC, False, True, False)

            pe.wait_ge(oh_done, 1)
            ohf = oh.rearrange("p t e -> p (t e)")
            pe.matmul(bankC[:, 0:P], cst[:, C_TRI], ohf, start=True, stop=True)
            pe.matmul(bankD[:, 0:P], ones, ohf, start=True, stop=True).then_inc(rank_mm, 1)
            for t in range(NT):
                pe.wait_ge(one_done, t // 4 + 1)
                mm = pe.matmul(bankC[:, 256:256 + SLOTW], one_row[:, t, :], one_slot[:, t, :], start=(t == 0), stop=(t == NT - 1))
            mm.then_inc(ids_mm, 1)

            pe.wait_ge(ids_done, 2)
            pe.wait_ge(w2_in_sem, 16)

            def turn_rows(j, turn):
                pe.wait_ge(e_in[j], 16 * (turn + 1))
                pe.transpose(bankA[:, 0:P], erow[:, j, HID:2 * HID], ident).then_inc(ezT_mm, 1)

            def first_layer(k, e):
                pe.wait_ge(ex_lo_done, k + 1)
                split3(bankU[0][0][:, :], ex_hi[:, :], ex_lo[:, :], w1_hi[:, ds(e * F, F)], w1_lo[:, ds(e * F, F)]).then_inc(h_mm, 1)

            def turn_hidden(k):
                pe.wait_ge(h_done, k + 1)
                for c in range(FC):
                    mm = pe.transpose(bankB[:, c * P:(c + 1) * P], hid[:, c * P:(c + 1) * P], ident)
                mm.then_inc(hT_mm, 1)

            def second_layer(k, e):
                pe.wait_ge(hT_done, k + 1)
                for c in range(FC):
                    mm = pe.matmul(bankU[1][0][:, 0:HID], hidT[:, c, :],
                                   w2[:, :, :, :].rearrange("p e c d -> p (e c d)")[:, ds(e * FC * HID + c * HID, HID)],
                                   start=(c == 0), stop=(c == FC - 1))
                mm.then_inc(y_mm, 1)

            def expert(k):
                return pe.value_load(expert_i[0:1, ds(k, 1)], min_val=0, max_val=E - 1)

            def tile(k, j, turn, has_prev, has_next):
                e = expert(k)
                e_prev = expert(k - 1) if has_prev else None
                first_layer(k, e)
                if has_next:
                    turn_rows((j + 1) % RING, turn + (j + 1) // RING)
                if has_prev:
                    if not (isinstance(k, int) and k == 1):
                        pe.wait_ge(eo_done, k - 1)
                    second_layer(k - 1, e_prev)
                turn_hidden(k)

            turn_rows(0, 0)
            for j in range(RING):
                tile(j, j, 0, j > 0, True)
            with pe.Fori(1, (SLOTS - 3) // RING) as m:
                for j in range(RING):
                    tile(m * RING + j, j, m, True, True)
            for j in range(3):
                tile(SLOTS - 3 + j, j, SLOTS // RING, True, j < 2)
            e = expert(SLOTS - 1)
            pe.wait_ge(eo_done, SLOTS - 1)
            second_layer(SLOTS - 1, e)

        @block.vector
        def _(eng):
            chain = {"base": 0, "n": 0}

            def link(ins):
                chain["n"] += 1
                ins.then_inc(dve, 1)
                eng.wait_ge(dve, chain["base"] + chain["n"])

            def merge_stats(st, mean, tmp, ve, eps):
                eng.tensor_tensor(tmp[0], st[:, :, 1], st[:, :, 4], ALU.subtract)
                eng.tensor_tensor(tmp[1], st[:, :, 2], st[:, :, 5], ALU.add)
                link(eng.tensor_tensor(tmp[2], st[:, :, 1], st[:, :, 4], ALU.add))
                link(eng.tensor_tensor(tmp[0], tmp[0], tmp[0], ALU.mult))
                eng.tensor_scalar(mean, tmp[2], 0.5, None, ALU.mult)
                link(eng.scalar_tensor_tensor(out=tmp[1], in0=tmp[0], scalar=P / 4.0, in1=tmp[1], op0=ALU.mult, op1=ALU.add))
                return eng.scalar_tensor_tensor(out=ve, in0=tmp[1], scalar=1.0 / P, in1=eps, op0=ALU.mult, op1=ALU.add)

            def two_stats(st, mean, ve, x_ap):
                for b in range(B):
                    ins = eng.bn_stats(st[:, b, :], x_ap[b])
                link(ins)
                return merge_stats(st, mean, [tmp_u[:, k, 0:B] for k in range(3)], ve, eps_row[:, 0:B])

            def x_stats(n):
                two_stats(st_x, mean_x, ve_x, [x_all[:, b, ds(n, 1), :].rearrange("p a d -> p (a d)") for b in range(B)]).then_inc(x_var, 1)

            def x_norm(n):
                eng.wait_ge(x_rstd, n + 1)
                for b in range(B):
                    ins = eng.tensor_scalar(xn[:, b, :], x_all[:, b, ds(n, 1), :].rearrange("p a d -> p (a d)"),
                                            mean_x[:, b:b + 1], rs_x[:, b:b + 1], ALU.subtract, ALU.mult)
                ins.then_inc(xn_done, 1)

            def x_low(n):
                eng.wait_ge(xT_hi_done, n + 1)
                eng.tensor_tensor(xT_lo[:, :, :].rearrange("p b t -> p (b t)"), bankA[:, 0:B * P],
                                  xT_hi[:, :, :].rearrange("p b t -> p (b t)").bitcast(F32), ALU.subtract).then_inc(xT_lo_done, 1)

            def rotate(n, i):
                eng.wait_ge(qk_mm, 4 * n + i + 1)
                src = ring[i][:, :].rearrange("p (h d) -> p h d", h=H)
                cos = cos_t[:, ds(n, 1), :].broadcast_to([P, H, D])
                eng.tensor_tensor(rot[:, i, :].rearrange("p (h d) -> p h d", h=H), src, cos, ALU.mult)
                if i >= 2:
                    eng.wait_ge(rot_add, 4 * n + i - 1)
                swapped = ring[i][:, :].rearrange("p (h s d) -> p h s d", h=H, s=2)[:, :, ::-1, :]
                sin = sin_t[:, ds(n, 1), :].rearrange("p a (s d) -> p a s d", s=2).broadcast_to([P, H, 2, D // 2])
                eng.tensor_tensor(rot_sin[:, i % 2, :].rearrange("p (h s d) -> p h s d", h=H, s=2), swapped, sin,
                                  ALU.mult).then_inc(rot_mul, 1)

            def weigh_v(n, i):
                eng.wait_ge(v_mm, 4 * n + i + 1)
                h0 = 4 * (i % 2)
                eng.tensor_tensor(vg[:, i // 2, h0 * V:(h0 + 4) * V].rearrange("p (h v) -> p h v", h=4),
                                  ring[i][:, :].rearrange("p (h v) -> p h v", h=4),
                                  cst[:, C_GV][:, h0:h0 + 4].unsqueeze(2).broadcast_to([P, 4, V]), ALU.mult).then_inc(v_done, 1)

            SC = [[bankB, bankC], [bankD, bankA]]

            def head_stats(n, b):
                eng.wait_ge(u_mm, 2 * n + b + 1)
                for h in range(H):
                    ins = eng.bn_stats(st_u[:, b, h, :], bankU[b][h % 2][:, (h // 2) * V:(h // 2 + 1) * V])
                link(ins)
                merge_stats(st_u[:, b, :, :], mean_u[:, b, :], [tmp_u[:, k, :] for k in range(3)], ve_u[:, b, :],
                            cst[:, C_EPS]).then_inc(u_var, 1)

            def head_norm(n, b):
                eng.wait_ge(u_rstd, 2 * n + b + 1)
                for h in range(H):
                    ins = eng.tensor_scalar(z[:, b, h * V:(h + 1) * V], bankU[b][h % 2][:, (h // 2) * V:(h // 2 + 1) * V],
                                            mean_u[:, b, h:h + 1], rs_u[:, b, h:h + 1], ALU.subtract, ALU.mult)
                ins.then_inc(z_done, 1)

            def state_add(n, b, has_prev):
                eng.wait_ge(st_mm, 2 * n + b + 1)
                bank = [bankC, bankD][b]
                if has_prev:
                    for p in range(HP):
                        s = slice(p * V, (p + 1) * V)
                        ins = eng.scalar_tensor_tensor(out=state[:, b, s], in0=state[:, b, s], scalar=cst[:, C_GC][:, p:p + 1],
                                                       in1=bank[:, s], op0=ALU.mult, op1=ALU.add)
                else:
                    ins = eng.tensor_copy(state[:, b, :], bank[:, :])
                ins.then_inc(st_done, 1)

            def step(n, has_cur, has_prev, has_next):
                if has_cur:
                    if has_prev:
                        eng.wait_ge(st_mm, 2 * n)
                    for i in range(4):
                        rotate(n, i)
                if has_next:
                    x_stats(n + 1)
                if has_cur:
                    for i in range(4):
                        weigh_v(n, i)
                if has_next:
                    x_norm(n + 1)
                if has_cur:
                    eng.wait_ge(w1_hi_done, n + 1)
                    eng.tensor_tensor(w1_lo[:, ds(n * F, F)], w1_stage[:, :], w1_hi[:, ds(n * F, F)].bitcast(F32),
                                      ALU.subtract).then_inc(w1_lo_done, 1)
                if has_next:
                    x_low(n + 1)
                if has_cur:
                    for b in range(B):
                        for par in range(2):
                            eng.wait_ge(sc_mm, 4 * n + 2 * b + par + 1)
                            eng.tensor_tensor(prob[:, b, par, :], SC[b][par][:, :], mask_t[:, par, :], ALU.mult).then_inc(sc_done, 1)
                if has_prev:
                    eng.wait_ge(wo_mm, n)
                    eng.tensor_tensor(x2[:, :, :], x_all[:, :, ds(n - 1, 1), :].rearrange("p b a d -> p b (a d)"),
                                      bankB[:, 0:B * HID].rearrange("p (b d) -> p b d", b=B), ALU.add).then_inc(x2_done, 1)
                    eng.wait_ge(x2_done, n)
                    two_stats(st_z, mean_z, ve_z, [x2[:, b, :] for b in range(B)]).then_inc(z_var, 1)
                    eng.wait_ge(z_rstd, 2 * n - 1)
                    for b in range(B):
                        ins = eng.tensor_scalar(z2[:, b, :], x2[:, b, :], mean_z[:, b:b + 1], rs_z[:, b:b + 1], ALU.subtract, ALU.mult)
                    ins.then_inc(z2_done, 1)
                    eng.wait_ge(z2_done, n)
                    two_stats(st_z, mean_z, ve_z, [z2[:, b, :] for b in range(B)]).then_inc(z_var, 1)
                    eng.wait_ge(z_rstd, 2 * n)
                    for b in range(B):
                        ins = eng.tensor_scalar(rows[:, b, HID:2 * HID], z2[:, b, :], mean_z[:, b:b + 1], rs_z[:, b:b + 1],
                                                ALU.subtract, ALU.mult)
                    ins.then_inc(rn_done, 1)
                if has_cur:
                    head_stats(n, 0)
                    head_stats(n, 1)
                    head_norm(n, 0)
                    if has_next:
                        state_add(n, 0, has_prev)
                    head_norm(n, 1)
                    if has_next:
                        state_add(n, 1, has_prev)
                if has_prev:
                    eng.wait_ge(pay_out, 16 * n)

            eng.memset(eps_row, EPS)
            eng.wait_ge(x_in_sem, 16)
            x_stats(0)
            x_norm(0)
            for i in range(3):
                eng.wait_ge(w_hi_done, i + 1)
                s = slice(1024 * i, 1024 * i + 1024)
                eng.tensor_tensor(w_lo[:, s], w_raw[:, s], w_hi[:, s].bitcast(F32), ALU.subtract).then_inc(w_lo_done, 1)
                if i == 0:
                    x_low(0)
            eng.wait_ge(c_in[0], 16)
            eng.wait_ge(c_in[1], 16)
            step(0, True, False, True)
            links = 3 * 4 + 2 * 4
            base = chain["n"]
            with eng.Fori(1, NC - 1) as n:
                chain.update(base=(n - 1) * links + base, n=0)
                step(n, True, True, True)
                assert chain["n"] == links, chain["n"]
            chain.update(base=(NC - 2) * links + base, n=0)
            step(NC - 1, True, True, False)
            step(NC, False, True, False)

            def row(ap):
                return ap.unsqueeze(2).broadcast_to([P, NT, E])

            def per_expert(ap):
                return ap.unsqueeze(1).broadcast_to([P, NT, E])

            eng.memset(ones, 1.0)
            eng.memset(scan0[:, 0:8, :], 0.0)
            eng.memset(scan1[:, 0:8, :], 0.0)
            eng.memset(zero8, 0.0)
            eng.wait_ge(lg_done, NC + 1)
            lg = logit[:, :, :, :].rearrange("p n b e -> p (n b) e")
            link(eng.tensor_reduce(mx, lg, AX.X, ALU.max))
            link(eng.tensor_tensor(eq, lg, row(mx), ALU.is_ge))
            link(eng.tensor_tensor(eq, eq, per_expert(cst[:, C_FIRST]), ALU.mult))
            link(eng.tensor_reduce(mw, eq, AX.X, ALU.max))
            eng.tensor_tensor(oh, eq, row(mw), ALU.is_equal).then_inc(oh_done, 1)
            eng.wait_ge(rank_mm, 1)
            link(eng.tensor_copy(scan0[:, 8:24, :], bankD[:, 0:P].rearrange("p (t e) -> p t e", t=NT)))
            src, dst = scan0, scan1
            for shift in (1, 2, 4, 8):
                link(eng.tensor_tensor(dst[:, 8:24, :], src[:, 8:24, :], src[:, 8 - shift:24 - shift, :], ALU.add))
                src, dst = dst, src
            link(eng.tensor_tensor(over, src[:, 23, :].unsqueeze(2).broadcast_to([P, E, NT]),
                                   cst[:, C_STEP].unsqueeze(1).broadcast_to([P, E, NT]), ALU.is_gt))
            link(eng.tensor_reduce(ntile, over, AX.X, ALU.add))
            link(eng.tensor_tensor_scan(tile_end, ntile, zero8, 0.0, ALU.add, ALU.add))
            link(eng.tensor_tensor(tile_start, tile_end, ntile, ALU.subtract))
            link(eng.scalar_tensor_tensor(out=place, in0=per_expert(tile_start), scalar=float(P), in1=src[:, 7:23, :],
                                          op0=ALU.mult, op1=ALU.add))
            link(eng.tensor_tensor(place, place, bankC[:, 0:P].rearrange("p (t e) -> p t e", t=NT), ALU.add))
            link(eng.tensor_tensor(place, place, oh, ALU.mult))
            link(eng.tensor_reduce(pos, place, AX.X, ALU.add))
            link(eng.tensor_copy(pos_i, pos))
            eng.tensor_scalar(slot_i, pos_i, 7, None, ALU.logical_shift_right)
            link(eng.tensor_scalar(row_i, pos_i, P - 1, None, ALU.bitwise_and))
            eng.tensor_copy(slot_f, slot_i)
            link(eng.tensor_copy(row_f, row_i))
            link(eng.tensor_tensor(one_slot, cst[:, C_SLOT].unsqueeze(1).broadcast_to([P, NT, SLOTW]),
                                   slot_f.unsqueeze(2).broadcast_to([P, NT, SLOTW]), ALU.is_equal))
            eng.tensor_tensor(one_slot, one_slot, cst[:, C_TOK].unsqueeze(2).broadcast_to([P, NT, SLOTW]), ALU.mult)
            for t in range(0, NT, 4):
                eng.tensor_tensor(one_row[:, t:t + 4, :], cst[:, C_IOTA].unsqueeze(1).broadcast_to([P, 4, P]),
                                  row_f[:, t:t + 4].unsqueeze(2).broadcast_to([P, 4, P]), ALU.is_equal).then_inc(one_done, 1)
            link(eng.tensor_tensor(below, tile_end[0:1, :].unsqueeze(1).broadcast_to([1, SLOTW, E]),
                                   cst[0:1, C_SLOT].unsqueeze(2).broadcast_to([1, SLOTW, E]), ALU.is_le))
            link(eng.tensor_reduce(expert_f, below, AX.X, ALU.add))
            eng.tensor_scalar(expert_i[:, :], expert_f, float(E - 1), None, ALU.min).then_inc(ids_done, 1)
            eng.wait_ge(ids_mm, 1)
            link(eng.tensor_copy(ids, bankC[:, 256:256 + SLOTW]))
            eng.tensor_scalar(gather_i[:, :], ids, -1.0, 0.0, ALU.add, ALU.max)
            link(eng.tensor_scalar(empty, ids, 0.0, float(PAD_ROW), ALU.is_equal, ALU.mult))
            eng.scalar_tensor_tensor(out=scatter_i[:, :], in0=ids, scalar=-1.0, in1=empty, op0=ALU.add,
                                     op1=ALU.add).then_inc(ids_done, 1)

            eng.wait_ge(ids_done, 2)
            eng.wait_ge(b_in[0], 16)

            def expert(k):
                return eng.value_load(expert_i[0:1, ds(k, 1)], min_val=0, max_val=E - 1)

            def rows_affine(k, e):
                eng.wait_ge(ezT_mm, k + 1)
                eng.tensor_scalar(exT, bankA[:, 0:P], lng[:, ds(e, 1)], lnb[:, ds(e, 1)], ALU.mult, ALU.add).then_inc(exT_done, 1)
                eng.wait_ge(ex_hi_done, k + 1)
                eng.tensor_tensor(ex_lo[:, :], exT, ex_hi[:, :].bitcast(F32), ALU.subtract).then_inc(ex_lo_done, 1)

            def tile(k, j, has_prev, has_next, stored=None):
                e = expert(k)
                if has_next:
                    rows_affine(k + 1, expert(k + 1))
                if stored is not None and j > 0:
                    eng.wait_ge(e_out[j - 1], stored)
                if stored is not None and j == RING - 1:
                    eng.wait_ge(e_out[j], stored)
                eng.wait_ge(h_mm, k + 1)
                eng.tensor_tensor(hid, bankU[0][0][:, :], b1_rep[:, ds(e * F, F)], ALU.add).then_inc(h_done, 1)
                if has_prev:
                    finish(k - 1, (j - 1) % RING)

            def finish(k, j, turn=None):
                eng.wait_ge(y_mm, k + 1)
                eng.wait_ge(resid_done, k + 1)
                eng.tensor_tensor(eout[:, j, :], bankU[1][0][:, 0:HID], resid, ALU.add).then_inc(eo_done, 1)

            rows_affine(0, expert(0))
            for j in range(RING):
                tile(j, j, j > 0, True)
            with eng.Fori(1, (SLOTS - 3) // RING) as m:
                for j in range(RING):
                    tile(m * RING + j, j, True, True, 16 * m)
            for j in range(3):
                tile(SLOTS - 3 + j, j, True, j < 2, 16 * (SLOTS // RING))
            eng.wait_ge(e_out[2], 16 * (SLOTS // RING))
            finish(SLOTS - 1, (SLOTS - 1) % RING)


def kernel(L0_attn_x, L0_attn_Wq, L0_attn_Wk, L0_attn_Wv, L0_attn_Wg, L0_attn_Wo, L0_attn_gn_weight, L0_attn_gn_bias,
           L0_ffn_centroids, L0_ffn_ln_g, L0_ffn_ln_b, L0_ffn_W1, L0_ffn_b1, L0_ffn_W2, L0_ffn_b2):
    import concourse.bacc as bacc
    from concourse.bass_utils import run_bass_kernel_spmd

    def a(v):
        return np.asarray(v)

    c = np.ascontiguousarray
    ins = {
        "x": c(a(L0_attn_x)),
        "wqkvg": c(np.concatenate([a(w) for w in (L0_attn_Wg, L0_attn_Wq, L0_attn_Wk, L0_attn_Wv)], 0).T),
        "wo": c(a(L0_attn_Wo).reshape(HID, H, V).transpose(2, 1, 0)),
        "gn": c(np.stack([a(L0_attn_gn_weight), a(L0_attn_gn_bias)]).reshape(2, H, V).transpose(2, 0, 1)),
        "cen": c(a(L0_ffn_centroids).T),
        "lng": c(a(L0_ffn_ln_g).T),
        "lnb": c(a(L0_ffn_ln_b).T),
        "w1": c(a(L0_ffn_W1).transpose(1, 0, 2)),
        "b1": c(a(L0_ffn_b1).reshape(-1)),
        "w2": c(a(L0_ffn_W2).reshape(E, FC, P, HID).transpose(2, 0, 1, 3)),
        "b2": c(a(L0_ffn_b2).reshape(-1)),
        "constants": constants(),
    }
    nc = bacc.Bacc("TRN2", target_bir_lowering=False, num_devices=1)
    args = [nc.dram_tensor(f"in_{n}", v.shape, mybir.dt.from_np(v.dtype), kind="ExternalInput").ap() for n, v in ins.items()]
    out = nc.dram_tensor("out", (B, T, HID), F32, kind="ExternalOutput").ap()
    preln_retention_moe_kernel(nc, *args, out)
    r = run_bass_kernel_spmd(nc, [{f"in_{n}": v for n, v in ins.items()}], core_ids=[0])
    return r.results[0]["out"]
```

```python
from contextlib import ExitStack

import numpy as np

import concourse.bass as bass
from concourse import mybir

F32 = mybir.dt.float32
F32R = mybir.dt.float32r
I32 = mybir.dt.int32
U32 = mybir.dt.uint32
ALU = mybir.AluOpType
ACT = mybir.ActivationFunctionType
AX = mybir.AxisListType
ds = bass.ds

P = 128
B, T, HID = 2, 1024, 128
H, D, V = 8, 64, 128
NC = T // P
HP = H // 2
E, F = 8, 512
FC = F // P
EPS = 1e-5
NTOK = B * T
NT = NTOK // P
SLOTS = NT + E - 1
SLOTW = 24
QT = NT
COLS = E * QT + 8
RING = 4
PAD_ROW = 4096

_at = 0


def _col(n):
    global _at
    _at += n
    return slice(_at - n, _at)


C_ID = _col(P)
C_COS = _col(NC * D)
C_SIN = _col(NC * D)
C_GV = _col(H)
C_EPS = _col(H)
C_GCV = _col(HP * V)
C_MASK = _col(H * P)
C_TRI = _col(P)
C_IOTA = _col(P)
C_SLOT = _col(SLOTW)
C_FIRST = _col(E)
C_STEP = _col(NT)
C_TOK = _col(NT + B)
C_ONES = _col(P)
C_ALL = _at


def constants():
    c = np.zeros((P, C_ALL), np.float32)
    i = np.arange(P)
    c[:, C_ID] = np.eye(P)
    inv = (np.float32(1.0) / np.float32(10000.0) ** (np.arange(0, D, 2, dtype=np.float32) / np.float32(D))).astype(np.float32)
    ang = np.arange(T, dtype=np.float32)[:, None] * inv[None, :]
    cos = np.concatenate([np.cos(ang), np.cos(ang)], 1)
    sin = np.concatenate([-np.sin(ang), np.sin(ang)], 1)
    c[:, C_COS] = cos.reshape(NC, P, D).transpose(1, 0, 2).reshape(P, -1)
    c[:, C_SIN] = sin.reshape(NC, P, D).transpose(1, 0, 2).reshape(P, -1)
    gamma = 1.0 - 2.0 ** (-5.0 - np.arange(H, dtype=np.float64))
    c[:, C_GV] = gamma[None, :] ** (P - i)[:, None]
    c[:, C_EPS] = D * EPS * gamma[None, :] ** (-2.0 * i)[:, None]
    for half in range(2):
        c[half * D:(half + 1) * D, C_GCV] = np.repeat(gamma[half::2] ** P, V)
    causal = (i[None, :] >= i[:, None]).astype(np.float64)
    order = [2 * p + half for half in range(2) for p in range(HP)]
    c[:, C_MASK] = (causal[:, None, :] * gamma[order][None, :, None] ** -i[:, None, None].astype(np.float64)).reshape(P, -1)
    c[:, C_TRI] = i[:, None] < i[None, :]
    c[:, C_IOTA] = i
    c[:, C_SLOT] = np.arange(SLOTW)
    c[:, C_FIRST] = E - np.arange(E)
    c[:, C_STEP] = P * np.arange(NT)
    tok = (np.arange(B)[None, None, :] * T + np.arange(NC)[None, :, None] * P + i[:, None, None]) + 1
    c[:, C_TOK][:, B:] = tok.reshape(P, NT)
    c[:, C_ONES] = 1.0
    return c


def preln_retention_moe_kernel(nc, x_in, wqkvg_in, wo_in, gn_in, cen_in, lng_in, lnb_in,
                               w1_in, b1_in, w2_in, b2_in, const_in, out):
    ctx = ExitStack()
    with ctx:
        def sb(name, shape, dt=F32):
            return ctx.enter_context(nc.sbuf_tensor(name, shape, dt))

        def sem(name):
            return ctx.enter_context(nc.semaphore(name))

        payload = nc.dram_tensor("payload", (NTOK, 2 * HID), F32, kind="Internal").ap()

        cst = sb("cst", [P, C_ALL])
        x_all = sb("x_all", [P, B, NC, HID])
        w_raw = sb("w_raw", [P, E * F])
        w_hi = sb("w_hi", [P, 3072], F32R)
        w_lo = sb("w_lo", [P, 3072], F32R)
        wo = sb("wo", [P, H, HID])
        gn = sb("gn", [P, 2, H])
        cen = sb("cen", [P, E])
        lng = sb("lng", [P, E])
        lnb = sb("lnb", [P, E])
        w1_stage = sb("w1_stage", [P, F])
        w1_hi = sb("w1_hi", [P, E * F], F32R)
        w1_lo = sb("w1_lo", [P, E * F], F32R)
        w2 = sb("w2", [P, E, FC, HID])
        b2_rep = sb("b2_rep", [P, E * HID])
        b1_rep = w_raw

        xn = sb("xn", [P, B, HID])
        xT_hi = sb("xT_hi", [P, B, P], F32R)
        xT_lo = sb("xT_lo", [P, B, P], F32R)
        rot = sb("rot", [P, 4, 512])
        rot_sin = sb("rot_sin", [P, 2, 512])
        kg = sb("kg", [P, B, 512])
        v_sb = sb("v_sb", [P, B, H * V])
        qkT = sb("qkT", [P, 4, 512])
        prob = sb("prob", [P, B, 2, 512])
        state = sb("state", [P, B, HP * V])
        z = sb("z", [P, B, H * V])
        sg = sb("sg", [P, 2, H, B * P])
        yT = sb("yT", [P, H, B * P])
        x2 = sb("x2", [P, B, HID])
        z2 = sb("z2", [P, B, HID])
        z2T = sb("z2T", [P, B, P])
        rows = sb("rows", [P, B, 2 * HID])
        logit = sb("logit", [P, B, E])
        half_row = sb("half_row", [P, NT])
        small = sb("small", [P, 256])

        st_x = sb("st_x", [P, NT, 6])
        mean_x, ve_x, rs_x, nb_x = [small[:, 16 * k:16 * k + 16] for k in range(4)]
        tmp_x = [small[:, 64 + 16 * k:80 + 16 * k] for k in range(3)]
        st_z = small[:, 112:124].rearrange("p (g s) -> p g s", g=B)
        var_z, mean_z, rs_z, rs2_z, pool_z, nb_z = [small[:, 124 + 2 * k:126 + 2 * k] for k in range(6)]
        tmp_z = [small[:, 136 + 2 * k:138 + 2 * k] for k in range(3)]
        eps_x = small[:, 142:158]
        st_u = sb("st_u", [P, B, H, 6])
        ve_u, rs_u, mean_u, nb_u = [small[:, 158 + 16 * k:174 + 16 * k].rearrange("p (b h) -> p b h", b=B) for k in range(4)]
        tmp_u = [small[:, 222 + 8 * k:230 + 8 * k] for k in range(3)]

        bankA, bankB, bankC, bankD = [ctx.enter_context(nc.psum_tensor(f"bank{c}", [P, 512], F32)) for c in "ABCD"]
        ring = [bankA, bankB, bankC, bankD]
        bankU = [[ctx.enter_context(nc.psum_tensor(f"bankU{b}{par}", [P, 512], F32)) for par in range(2)] for b in range(B)]

        route = sb("route", [P, 128])
        best, first, rank, tile_f, row_f = [route[:, 2 * k:2 * k + 2] for k in range(5)]
        eq, chosen, before, placed = [route[:, 16 + 16 * k:32 + 16 * k].rearrange("p (b e) -> p b e", b=B) for k in range(4)]
        same_tile = sb("same_tile", [P, B, QT])[:, :, :]
        ntile, tile_end, zero8 = route[:, 80:88], route[:, 88:96], route[:, 96:104]
        rank_i = sb("rank_i", [P, 6], I32)
        one_row = sb("one_row", [P, B, P])
        one_tile = sb("one_tile", [P, B, E, QT])
        ids = sb("ids", [P, E * QT])
        plan = rot_sin[:, :, :].rearrange("p a n -> p (a n)")
        over = plan[:, 0:128].rearrange("p (e j) -> p e j", e=E)
        empty = plan[:, 0:128]
        below = plan[0:1, 128:320].rearrange("p (k e) -> p k e", e=E)
        passed, used = plan[0:1, 320:344], plan[0:1, 344:368]
        table = plan[:, 512:512 + 2 * COLS].bitcast(U32).rearrange("p (c k) -> p c k", k=2)
        at = sb("at", [P, 2 * RING, 2], U32)
        zero_u = sb("zero_u", [P, 2], U32)
        expert_i = sb("expert_i", [1, SLOTW], I32)
        col_i = sb("col_i", [1, SLOTW], I32)

        sgf = sg[:, :, :, :].rearrange("p a h n -> p (a h n)")
        erow = sgf[:, 0:1024].rearrange("p (r n) -> p r n", r=RING)
        eout = sgf[:, 1024:1536].rearrange("p (r n) -> p r n", r=RING)
        resid = sgf[:, 1536:2048].rearrange("p (r n) -> p r n", r=RING)
        exT = sgf[:, 2048:2048 + P]
        hid = sgf[:, 2560:3072]
        hidT = sgf[:, 3072:3584].rearrange("p (c t) -> p c t", c=FC)
        ex_hi, ex_lo = xT_hi, xT_lo

        ident = cst[:, C_ID]
        cos_t = cst[:, C_COS].rearrange("p (n d) -> p n d", d=D)
        sin_t = cst[:, C_SIN].rearrange("p (n d) -> p n d", d=D)
        mask_t = cst[:, C_MASK].rearrange("p (a n) -> p a n", a=2)

        x_in_sem = sem("x_in_sem")
        c_in = [sem(f"c_in{i}") for i in range(2)]
        w_in = [sem(f"w_in{i}") for i in range(3)]
        small_in = sem("small_in")
        wo_in_sem = sem("wo_in_sem")
        w1_in_sem = sem("w1_in_sem")
        w2_in_sem = sem("w2_in_sem")
        b_in = [sem("b1_in_sem"), sem("b2_in_sem")]
        w_hi_done, w_lo_done = sem("w_hi_done"), sem("w_lo_done")
        w1_hi_done, w1_lo_done = sem("w1_hi_done"), sem("w1_lo_done")
        x_var, x_rstd, x_nb = sem("x_var"), sem("x_rstd"), sem("x_nb")
        xn_done = sem("xn_done")
        xT_mm, xT_hi_done, xT_lo_done = sem("xT_mm"), sem("xT_hi_done"), sem("xT_lo_done")
        g_mm, sg_done = sem("g_mm"), sem("sg_done")
        qk_mm, rot_mul, rot_add = sem("qk_mm"), sem("rot_mul"), sem("rot_add")
        v_mm, v_done = sem("v_mm"), sem("v_done")
        qkT_mm, qkT_done = sem("qkT_mm"), sem("qkT_done")
        sc_mm, sc_done = sem("sc_mm"), sem("sc_done")
        u_mm, u_var, u_rstd, z_done = sem("u_mm"), sem("u_var"), sem("u_rstd"), sem("z_done")
        kg_done, decayed, st_mm, st_done = sem("kg_done"), sem("decayed"), sem("st_mm"), sem("st_done")
        zT_mm, za_done, y_done = sem("zT_mm"), sem("za_done"), sem("y_done")
        wo_mm, x2_done = sem("wo_mm"), sem("x2_done")
        z_var, z_rstd, z_nb, z2_done, rn_done, rs_done = (sem(n) for n in ("z_var", "z_rstd", "z_nb", "z2_done", "rn_done", "rs_done"))
        z2T_mm, z2T_done, lg_mm, lg_done = sem("z2T_mm"), sem("z2T_done"), sem("lg_mm"), sem("lg_done")
        pay_out = sem("pay_out")
        dve = sem("dve_chain")
        pool_init, pool_chain = sem("pool_init"), sem("pool_chain")
        chosen_done, rank_mm, rank_read, one_done, ids_mm, ids_add = (
            sem(n) for n in ("chosen_done", "rank_mm", "rank_read", "one_done", "ids_mm", "ids_add"))
        plan_done, table_done = sem("plan_done"), sem("table_done")
        row_placed = sem("row_placed")
        e_in = [sem(f"e_in{i}") for i in range(RING)]
        e_out = [sem(f"e_out{i}") for i in range(RING)]
        ezT_mm, exT_done, ex_hi_done, ex_lo_done = (sem(n) for n in ("ezT_mm", "exT_done", "ex_hi_done", "ex_lo_done"))
        h_mm, h_done, hT_mm, hT_done = (sem(n) for n in ("h_mm", "h_done", "hT_mm", "hT_done"))
        y_mm, eo_done, resid_done = (sem(n) for n in ("y_mm", "eo_done", "resid_done"))

        block = ctx.enter_context(nc.Block())

        @block.sync
        def _(sp):
            sp.dma_start(x_all[:, :, :, :], x_in.rearrange("b (n p) d -> p b n d", p=P)).then_inc(x_in_sem, 16)
            for i in range(3):
                sp.dma_start(w_raw[:, 1024 * i:1024 * i + 1024], wqkvg_in[:, 1024 * i:1024 * i + 1024]).then_inc(w_in[i], 16)
                if i == 0:
                    sp.dma_start(cst[:, 0:C_GCV.start], const_in[:, 0:C_GCV.start]).then_inc(c_in[0], 16)
            sp.dma_start(cst[:, C_GCV.start:C_ALL], const_in[:, C_GCV.start:C_ALL]).then_inc(c_in[1], 16)
            sp.dma_start(gn[:, :, :], gn_in).then_inc(small_in, 16)
            sp.dma_start(cen[:, :], cen_in).then_inc(small_in, 16)
            sp.dma_start(lng[:, :], lng_in).then_inc(small_in, 16)
            sp.dma_start(lnb[:, :], lnb_in).then_inc(small_in, 16)
            sp.dma_start(wo[:, :, :], wo_in).then_inc(wo_in_sem, 16)
            sp.dma_start(w1_stage[:, :], w1_in[:, 0, :]).then_inc(w1_in_sem, 16)
            sp.dma_start(w2[:, :, :, :], w2_in).then_inc(w2_in_sem, 16)
            sp.dma_start(b2_rep[:, :], b2_in.partition_broadcast(P)).then_inc(b_in[1], 16)
            sp.wait_ge(w_lo_done, 3)
            sp.dma_start(b1_rep[:, :], b1_in.partition_broadcast(P)).then_inc(b_in[0], 16)

            def step(n):
                sp.wait_ge(w1_lo_done, n)
                sp.dma_start(w1_stage[:, :], w1_in[:, ds(n, 1), :].rearrange("p a f -> p (a f)")).then_inc(w1_in_sem, 16)

            def store_rows(n):
                sp.wait_ge(rn_done, n)
                sp.wait_ge(rs_done, n)
                sp.dma_start(payload.rearrange("(b n p) c -> p b n c", b=B, p=P)[:, :, ds(n - 1, 1), :]
                             .rearrange("p b a c -> p b (a c)"), rows[:, :, :]).then_inc(pay_out, 16)

            with sp.Fori(1, NC) as n:
                step(n)
                store_rows(n)
            store_rows(NC)

        @block.gpsimd
        def _(pool):
            chain = {"base": 0, "n": 0}

            def link(ins):
                chain["n"] += 1
                ins.then_inc(pool_chain, 1)
                pool.wait_ge(pool_chain, chain["base"] + chain["n"])

            pool.memset(half_row[:, :], -0.5).then_inc(pool_init, 1)
            pool.memset(logit[:, :, :], 0.0).then_inc(lg_done, 1)
            pool.memset(zero_u[:, :], 0).then_inc(pool_init, 1)
            pool.wait_ge(pool_init, 2)

            def rstd(out_ap, in_ap):
                return pool.tensor_tensor(out_ap, in_ap, half_row[:, 0:in_ap.shape[1]], ALU.pow)

            def rstd_heads(n, b):
                pool.wait_ge(u_var, 2 * n + b + 1)
                link(rstd(rs_u[:, b, :], ve_u[:, b, :]))
                pool.tensor_tensor(nb_u[:, b, :], mean_u[:, b, :], rs_u[:, b, :], ALU.mult).then_inc(u_rstd, 1)

            def decay_state(n, b):
                pool.wait_ge(u_mm, 2 * n + b + 1)
                pool.tensor_tensor(state[:, b, :], state[:, b, :], cst[:, C_GCV], ALU.mult).then_inc(decayed, 1)

            def step(n, has_cur, has_prev, has_next):
                if has_cur:
                    for i in range(4):
                        pool.wait_ge(rot_mul, 4 * n + i + 1)
                        pool.tensor_tensor(rot[:, i, :], rot[:, i, :], rot_sin[:, i % 2, :], ALU.add).then_inc(rot_add, 1)
                if has_prev:
                    for j in range(4):
                        pool.wait_ge(za_done, 4 * n - 4 + j + 1)
                        y = yT[:, 2 * j:2 * j + 2, :].rearrange("p h n -> p (h n)")
                        pool.tensor_tensor(y, y, sg[:, ds((n - 1) % 2, 1), 2 * j:2 * j + 2, :].rearrange("p a h n -> p (a h n)"),
                                           ALU.mult).then_inc(y_done, 1)
                if has_next:
                    for b in range(B):
                        pool.wait_ge(rot_add, 4 * n + 2 * b + 2)
                        pool.tensor_tensor(kg[:, b, :].rearrange("p (h d) -> p h d", h=H),
                                           rot[:, 2 * b + 1, :].rearrange("p (h d) -> p h d", h=H),
                                           cst[:, C_GV].unsqueeze(2).broadcast_to([P, H, D]), ALU.mult).then_inc(kg_done, 1)
                if has_prev:
                    pool.wait_ge(z_var, n)
                    rs = rstd(rs_z, tmp_z[2])
                    rs.then_inc(z_rstd, 1)
                    pool.wait_ge(z_rstd, 2 * n - 1)
                    link(pool.tensor_tensor(pool_z, rs_z, rs_z, ALU.mult))
                    link(pool.tensor_tensor(pool_z, pool_z, var_z, ALU.mult))
                    link(pool.tensor_tensor(pool_z, pool_z, eps_x[:, 0:B], ALU.add))
                    rstd(rs2_z, pool_z).then_inc(z_rstd, 1)
                    pool.wait_ge(z2_done, n)
                    pool.tensor_tensor(rows[:, :, 0:HID], x2[:, :, :], z2[:, :, :], ALU.add).then_inc(rs_done, 1)
                if has_cur:
                    rstd_heads(n, 0)
                    if has_prev and has_next:
                        decay_state(n, 0)
                        decay_state(n, 1)
                    rstd_heads(n, 1)
                if has_prev:
                    pool.wait_ge(pay_out, 16 * n)

            pool.wait_ge(x_var, 1)
            link(rstd(rs_x, ve_x))
            pool.tensor_tensor(nb_x, mean_x, rs_x, ALU.mult).then_inc(x_nb, 1)
            step(0, True, False, True)
            links = 3 + 2
            base = chain["n"]
            with pool.Fori(1, NC - 1) as n:
                chain.update(base=(n - 1) * links + base, n=0)
                step(n, True, True, True)
                assert chain["n"] == links, chain["n"]
            chain.update(base=(NC - 2) * links + base, n=0)
            step(NC - 1, True, True, False)
            step(NC, False, True, False)

            pool.memset(table[:, E * QT:COLS, 0], 0).then_inc(pool_init, 1)
            pool.memset(table[:, E * QT:COLS, 1], PAD_ROW).then_inc(pool_init, 1)
            pool.wait_ge(pool_init, 4)
            last_token = pool.to_reg(NTOK - 1)

            def place(k, j, which):
                col = pool.value_load(col_i[0:1, ds(k, 1)], min_val=0, max_val=COLS - 1)
                return pool.tensor_tensor(at[:, j + RING * which, which:which + 1],
                                          table[:, ds(col, 1), which], zero_u[:, 0:1], ALU.add)

            def gather(j):
                pool.indirect_dma_start(out=erow[:, j, :], out_offset=None, in_=payload,
                                        in_offset=bass.IndirectOffsetOnAxis(ap=at[:, j, 0:1], axis=0),
                                        bounds_check=last_token, oob_is_err=False).then_inc(e_in[j], 16)

            def scatter(j):
                pool.indirect_dma_start(out=out.rearrange("b t d -> (b t) d"), in_=eout[:, j, :], in_offset=None,
                                        out_offset=bass.IndirectOffsetOnAxis(ap=at[:, j + RING, 1:2], axis=0),
                                        bounds_check=last_token, oob_is_err=False).then_inc(e_out[j], 16)

            def tile(k, j, turn, has_prev, has_gather, has_place):
                col_s = pool.value_load(col_i[0:1, ds(k, 1)], min_val=0, max_val=COLS - 1)
                if has_place:
                    col_g = pool.value_load(col_i[0:1, ds(k + 5, 1)], min_val=0, max_val=COLS - 1)
                    if has_gather:
                        pool.wait_ge(ezT_mm, k + 2)
                        pool.wait_ge(resid_done, k + 1)
                    pool.tensor_tensor(at[:, (j + 1) % RING, 0:1], table[:, ds(col_g, 1), 0], zero_u[:, 0:1],
                                       ALU.add).then_inc(row_placed, 1)
                elif has_gather:
                    pool.wait_ge(resid_done, k + 1)
                if has_prev:
                    pool.wait_ge(eo_done, k)
                if not (isinstance(turn, int) and turn == 0):
                    pool.wait_ge(e_out[j], 16 * turn)
                pool.wait_ge(row_placed, 2 * k + 5 if has_place else k + SLOTS)
                pool.tensor_tensor(at[:, j + RING, 1:2], table[:, ds(col_s, 1), 1], zero_u[:, 0:1], ALU.add).then_inc(row_placed, 1)
                if has_gather:
                    gather(j)
                if has_prev:
                    scatter((j - 1) % RING)

            pool.wait_ge(plan_done, 1)
            pool.wait_ge(table_done, 1)
            for j in range(RING):
                place(j, j, 0).then_inc(row_placed, 1)
                pool.wait_ge(row_placed, j + 1)
                if j == 0:
                    pool.wait_ge(pay_out, 16 * NC)
                gather(j)
            pool.wait_ge(e_in[0], 16)
            place(RING, 0, 0).then_inc(row_placed, 1)
            for j in range(RING):
                tile(j, j, 0, j > 0, True, True)
            with pool.Fori(1, (SLOTS - 7) // RING) as m:
                for j in range(RING):
                    tile(m * RING + j, j, m, True, True, True)
            for k in range(SLOTS - 7, SLOTS):
                tile(k, k % RING, k // RING, True, k + 4 < SLOTS, k + 5 < SLOTS)
            pool.wait_ge(row_placed, 2 * SLOTS)
            pool.wait_ge(eo_done, SLOTS)
            scatter((SLOTS - 1) % RING)
            for j in range(RING):
                pool.wait_ge(e_out[j], 16 * len(range(j, SLOTS, RING)))

        @block.scalar
        def _(act):
            def normalise_x(n):
                if isinstance(n, int) and n == 0:
                    act.wait_ge(x_nb, 1)
                else:
                    act.wait_ge(xT_mm, n)
                for b in range(B):
                    a = act.activation(xn[:, b, :], x_all[:, b, ds(n, 1), :].rearrange("p a d -> p (a d)"), ACT.Identity,
                                       scale=rs_x[:, ds(b * NC + n, 1)], bias=nb_x[:, ds(b * NC + n, 1)])
                a.then_inc(xn_done, 1)

            def x_high(n):
                act.wait_ge(xT_mm, n + 1)
                act.activation(xT_hi[:, :, :].rearrange("p b t -> p (b t)"), bankA[:, 0:B * P], ACT.Copy).then_inc(xT_hi_done, 1)

            def normalise_heads(n, b):
                act.wait_ge(u_rstd, 2 * n + b + 1)
                for h in range(H):
                    a = act.activation(z[:, b, h * V:(h + 1) * V], bankU[b][h % 2][:, (h // 2) * V:(h // 2 + 1) * V], ACT.Identity,
                                       scale=rs_u[:, b, h:h + 1], bias=nb_u[:, b, h:h + 1])
                a.then_inc(z_done, 1)

            def step(n, has_cur, has_prev, has_next):
                if has_cur:
                    for j in range(4):
                        act.wait_ge(g_mm, 4 * n + j + 1)
                        act.activation(sg[:, ds(n % 2, 1), 2 * j:2 * j + 2, :].rearrange("p a h n -> p (a h n)"),
                                       ring[j][:, :], ACT.Silu).then_inc(sg_done, 1)
                if has_prev:
                    normalise_heads(n - 1, 1)
                if has_cur:
                    for i in range(4):
                        act.wait_ge(v_mm, 4 * n + i + 1)
                        act.activation(v_sb[:, i // 2, 512 * (i % 2):512 * (i % 2) + 512], ring[i][:, :], ACT.Copy).then_inc(v_done, 1)
                if has_prev:
                    for j in range(4):
                        act.wait_ge(zT_mm, 4 * n - 4 + j + 1)
                        for h in (2 * j, 2 * j + 1):
                            a = act.activation(yT[:, h, :], ring[j][:, (h % 2) * 256:(h % 2) * 256 + 256], ACT.Identity,
                                               scale=gn[:, 0, h:h + 1], bias=gn[:, 1, h:h + 1])
                        a.then_inc(za_done, 1)
                if has_cur:
                    for i in range(4):
                        act.wait_ge(qkT_mm, 4 * n + i + 1)
                        act.activation(qkT[:, i, :], ring[i][:, :], ACT.Copy).then_inc(qkT_done, 1)
                        if i == 0 and has_next:
                            normalise_x(n + 1)
                if has_next:
                    x_high(n + 1)
                if has_cur:
                    act.wait_ge(w1_in_sem, 16 * n + 16)
                    act.activation(w1_hi[:, ds(n * F, F)], w1_stage[:, :], ACT.Copy).then_inc(w1_hi_done, 1)
                if has_prev:
                    act.wait_ge(z2T_mm, n)
                    act.activation(z2T[:, :, :].rearrange("p b t -> p (b t)"), bankA[:, 0:B * P], ACT.Copy).then_inc(z2T_done, 1)
                    act.wait_ge(lg_mm, n)
                    act.activation(logit[:, :, :].rearrange("p b e -> p (b e)"), bankB[:, 0:B * E], ACT.Copy).then_inc(lg_done, 1)
                if has_cur:
                    normalise_heads(n, 0)
                if has_prev:
                    act.wait_ge(y_done, 4 * n)

            normalise_x(0)
            for i in range(3):
                act.wait_ge(w_in[i], 16)
                act.activation(w_hi[:, 1024 * i:1024 * i + 1024], w_raw[:, 1024 * i:1024 * i + 1024], ACT.Copy).then_inc(w_hi_done, 1)
                if i == 0:
                    x_high(0)
            act.wait_ge(small_in, 64)
            step(0, True, False, True)
            with act.Fori(1, NC - 1) as n:
                step(n, True, True, True)
            step(NC - 1, True, True, False)
            step(NC, False, True, False)

            def high(k, j):
                act.wait_ge(exT_done, k + 1)
                act.activation(ex_hi[:, j % 2, :], exT, ACT.Copy).then_inc(ex_hi_done, 1)

            def tile(k, j, has_next2):
                if has_next2:
                    high(k + 2, j)
                act.wait_ge(hT_mm, k + 1)
                act.activation(hidT.rearrange("p c t -> p (c t)"), bankB[:, :], ACT.Relu).then_inc(hT_done, 1)

            high(0, 0)
            high(1, 1)
            tile(0, 0, True)
            with act.Fori(0, (SLOTS - 3) // 2) as m:
                for j in (1, 2):
                    tile(2 * m + j, j, True)
            tile(SLOTS - 2, 1, False)
            tile(SLOTS - 1, 0, False)

        @block.tensor
        def _(pe):
            def split3(out_ap, l_hi, l_lo, r_hi, r_lo):
                pe.matmul(out_ap, l_hi, r_hi, start=True, stop=False)
                pe.matmul(out_ap, l_hi, r_lo, start=False, stop=False)
                return pe.matmul(out_ap, l_lo, r_hi, start=False, stop=True)

            def x_turn(n):
                pe.wait_ge(xn_done, n + 1)
                for b in range(B):
                    mm = pe.transpose(bankA[:, b * P:(b + 1) * P], xn[:, b, :], ident)
                mm.then_inc(xT_mm, 1)

            def project(n, has_prev):
                pe.wait_ge(xT_lo_done, n + 1)
                for j in range(4):
                    if has_prev:
                        if j == 0:
                            pe.wait_ge(sc_done, 4 * n)
                            pe.wait_ge(ids_add, n)
                        elif j == 1:
                            pe.wait_ge(lg_done, n)
                        else:
                            pe.wait_ge(st_done, 2 * n - 3 + j)
                    for c in (2 * j, 2 * j + 1):
                        s = slice(c * P, (c + 1) * P)
                        mm = split3(ring[j][:, (c % 2) * 256:(c % 2) * 256 + 256], w_hi[:, s], w_lo[:, s],
                                    xT_hi[:, :, :].rearrange("p b t -> p (b t)"), xT_lo[:, :, :].rearrange("p b t -> p (b t)"))
                    mm.then_inc(g_mm, 1)
                if not has_prev:
                    pe.wait_ge(w_lo_done, 2)
                for i in range(4):
                    pe.wait_ge(sg_done, 4 * n + i + 1)
                    s = slice(1024 + 512 * (i % 2), 1536 + 512 * (i % 2))
                    split3(ring[i][:, :], xT_hi[:, i // 2, :], xT_lo[:, i // 2, :], w_hi[:, s], w_lo[:, s]).then_inc(qk_mm, 1)
                if not has_prev:
                    pe.wait_ge(w_lo_done, 3)
                for i in range(4):
                    pe.wait_ge(rot_mul, 4 * n + i + 1)
                    s = slice(2048 + 512 * (i % 2), 2560 + 512 * (i % 2))
                    split3(ring[i][:, :], xT_hi[:, i // 2, :], xT_lo[:, i // 2, :], w_hi[:, s], w_lo[:, s]).then_inc(v_mm, 1)

            def turn_z(n, has_cur):
                pe.wait_ge(z_done, 2 * n)
                for j in range(4):
                    if has_cur:
                        pe.wait_ge(v_done, 4 * n + j + 1)
                    elif j == 0:
                        pe.wait_ge(sc_done, 4 * n)
                        pe.wait_ge(ids_add, n)
                    elif j == 1:
                        pe.wait_ge(lg_done, n)
                    for h in (2 * j, 2 * j + 1):
                        for b in range(B):
                            c = (h % 2) * 256 + b * P
                            mm = pe.transpose(ring[j][:, c:c + P], z[:, b, h * V:(h + 1) * V], ident)
                    mm.then_inc(zT_mm, 1)

            def turn_qk(n, has_prev):
                for i in range(4):
                    pe.wait_ge(rot_add, 4 * n + i + 1)
                    if has_prev:
                        pe.wait_ge(za_done, 4 * n - 4 + i + 1)
                    else:
                        pe.wait_ge(v_done, 4 * n + i + 1)
                    for p in range(HP):
                        mm = pe.transpose(ring[i][:, p * P:(p + 1) * P], rot[:, i, p * P:(p + 1) * P], ident)
                    mm.then_inc(qkT_mm, 1)

            def rank_tokens(n):
                pe.wait_ge(chosen_done, n)
                o = bankA[:, 256:256 + B * E]
                pe.matmul(o, cst[:, C_TRI], chosen.rearrange("p b e -> p (b e)"), start=True, stop=False)
                pe.matmul(o, cst[:, C_ONES], before.rearrange("p b e -> p (b e)"), start=False, stop=True).then_inc(rank_mm, 1)

            def spread_tokens(n):
                pe.wait_ge(one_done, n)
                for b in range(B):
                    mm = pe.matmul(bankA[:, 256:256 + E * QT], one_row[:, b, :], one_tile[:, b, :, :].rearrange("p e q -> p (e q)"),
                                   start=(b == 0), stop=(b == B - 1))
                mm.then_inc(ids_mm, 1)

            SC = [[bankB, bankC], [bankD, bankA]]

            def scores(n, b, has_prev, has_next):
                pe.wait_ge(qkT_done, 4 * n + 2 * b + 2)
                if b == 0:
                    pe.wait_ge(qkT_done, 4 * n + 3)
                else:
                    pe.wait_ge(qkT_done, 4 * n + 4)
                    if has_next:
                        pe.wait_ge(xT_lo_done, n + 2)
                    if has_prev:
                        pe.wait_ge(rank_read, n)
                for h in range(H):
                    par, p = h % 2, h // 2
                    q = qkT[par * D:(par + 1) * D, 2 * b, p * P:(p + 1) * P]
                    k = qkT[par * D:(par + 1) * D, 2 * b + 1, p * P:(p + 1) * P]
                    mm = pe.matmul(SC[b][par][:, p * P:(p + 1) * P], k, q, start=True, stop=True)
                    if h >= H - 2:
                        mm.then_inc(sc_mm, 1)

            def project_out(n, has_cur):
                pe.wait_ge(y_done, 4 * n)
                if has_cur:
                    pe.wait_ge(sc_done, 4 * n + 1)
                for b in range(B):
                    for h in range(H):
                        mm = pe.matmul(bankB[:, b * HID:(b + 1) * HID], yT[:, h, b * P:(b + 1) * P], wo[:, h, :],
                                       start=(h == 0), stop=(h == H - 1))
                mm.then_inc(wo_mm, 1)

            def retain(n, b, has_prev):
                pe.wait_ge(sc_done, 4 * n + 2 * b + 2)
                if has_prev:
                    pe.wait_ge(z_done, 2 * n - 2 + b + 1)
                    pe.wait_ge(st_done, 2 * n - 2 + b + 1)
                for p in range(HP):
                    if has_prev:
                        for par in range(2):
                            hs = slice(par * D, (par + 1) * D)
                            pe.matmul(bankU[b][par][:, p * V:(p + 1) * V], qkT[hs, 2 * b, p * P:(p + 1) * P],
                                      state[hs, b, p * V:(p + 1) * V], start=True, stop=False)
                    for par in range(2):
                        h = 2 * p + par
                        mm = pe.matmul(bankU[b][par][:, p * V:(p + 1) * V], prob[:, b, par, p * P:(p + 1) * P],
                                       v_sb[:, b, h * V:(h + 1) * V], start=not has_prev, stop=True)
                mm.then_inc(u_mm, 1)

            def update_state(n, b):
                pe.wait_ge(kg_done, 2 * n + b + 1)
                for h in range(H):
                    par, p = h % 2, h // 2
                    mm = pe.matmul([bankC, bankD][b][par * D:(par + 1) * D, p * V:(p + 1) * V],
                                   kg[:, b, h * D:(h + 1) * D], v_sb[:, b, h * V:(h + 1) * V], start=True, stop=True)
                mm.then_inc(st_mm, 1)

            def turn_z2(n, has_cur):
                pe.wait_ge(z2_done, n)
                if has_cur:
                    pe.wait_ge(sc_done, 4 * n + 4)
                spread_tokens(n)
                for b in range(B):
                    mm = pe.transpose(bankA[:, b * P:(b + 1) * P], z2[:, b, :], ident)
                mm.then_inc(z2T_mm, 1)

            def logits(n):
                pe.wait_ge(z2T_done, n)
                pe.wait_ge(x2_done, n)
                for b in range(B):
                    mm = pe.matmul(bankB[:, b * E:(b + 1) * E], z2T[:, b, :], cen[:, :], start=True, stop=True)
                mm.then_inc(lg_mm, 1)

            def step(n, has_cur, has_prev, has_next):
                if has_cur:
                    project(n, has_prev)
                if has_prev:
                    turn_z(n, has_cur)
                if has_cur:
                    turn_qk(n, has_prev)
                    pe.wait_ge(qkT_done, 4 * n + 1)
                else:
                    pe.wait_ge(za_done, 4 * n - 3)
                if has_prev:
                    rank_tokens(n)
                if has_next:
                    x_turn(n + 1)
                if has_cur:
                    scores(n, 0, has_prev, has_next)
                    scores(n, 1, has_prev, has_next)
                if has_prev:
                    project_out(n, has_cur)
                if has_cur:
                    retain(n, 0, has_prev)
                    retain(n, 1, has_prev)
                if has_prev:
                    turn_z2(n, has_cur)
                if has_next:
                    update_state(n, 0)
                    update_state(n, 1)
                if has_prev:
                    logits(n)

            pe.wait_ge(c_in[0], 16)
            x_turn(0)
            pe.wait_ge(w_lo_done, 1)
            step(0, True, False, True)
            pe.wait_ge(c_in[1], 16)
            pe.wait_ge(wo_in_sem, 16)
            with pe.Fori(1, NC - 1) as n:
                step(n, True, True, True)
            step(NC - 1, True, True, False)
            step(NC, False, True, False)

            pe.wait_ge(chosen_done, NC + 1)
            for i, a in enumerate((before, chosen)):
                mm = pe.matmul(bankC[:, 0:E], cst[:, C_ONES], a[:, B - 1, :], start=(i == 0), stop=(i == 1))
            pe.wait_ge(ids_add, NC + 1)
            rank_tokens(NC + 1)
            spread_tokens(NC + 1)

            pe.wait_ge(plan_done, 1)
            pe.wait_ge(w2_in_sem, 16)

            def turn_rows(k, j, turn):
                pe.wait_ge(e_in[j], 16 * (turn + 1))
                if not (isinstance(k, int) and k == 0):
                    pe.wait_ge(exT_done, k)
                else:
                    pe.wait_ge(ids_add, NC + 2)
                pe.transpose(bankA[:, 0:P], erow[:, j, HID:2 * HID], ident).then_inc(ezT_mm, 1)

            def first_layer(k, j, e):
                pe.wait_ge(ex_lo_done, k + 1)
                split3(bankU[0][0][:, :], ex_hi[:, j % 2, :], ex_lo[:, j % 2, :], w1_hi[:, ds(e * F, F)],
                       w1_lo[:, ds(e * F, F)]).then_inc(h_mm, 1)

            def turn_hidden(k):
                pe.wait_ge(h_done, k + 1)
                for c in range(FC):
                    mm = pe.transpose(bankB[:, c * P:(c + 1) * P], hid[:, c * P:(c + 1) * P], ident)
                mm.then_inc(hT_mm, 1)

            def second_layer(k, e):
                pe.wait_ge(hT_done, k + 1)
                for c in range(FC):
                    mm = pe.matmul(bankU[1][0][:, 0:HID], hidT[:, c, :],
                                   w2[:, :, :, :].rearrange("p e c d -> p (e c d)")[:, ds(e * FC * HID + c * HID, HID)],
                                   start=(c == 0), stop=(c == FC - 1))
                mm.then_inc(y_mm, 1)

            def expert(k):
                return pe.value_load(expert_i[0:1, ds(k, 1)], min_val=0, max_val=E - 1)

            def tile(k, j, turn, has_prev, has_next2):
                e = expert(k)
                e_prev = expert(k - 1) if has_prev else None
                first_layer(k, j, e)
                if has_next2:
                    turn_rows(k + 2, (j + 2) % RING, turn + (j + 2) // RING)
                if has_prev:
                    if not (isinstance(k, int) and k == 1):
                        pe.wait_ge(eo_done, k - 1)
                    second_layer(k - 1, e_prev)
                turn_hidden(k)

            turn_rows(0, 0, 0)
            turn_rows(1, 1, 0)
            for j in range(RING):
                tile(j, j, 0, j > 0, True)
            with pe.Fori(1, (SLOTS - 3) // RING) as m:
                for j in range(RING):
                    tile(m * RING + j, j, m, True, True)
            for j in range(3):
                tile(SLOTS - 3 + j, j, SLOTS // RING, True, j < 1)
            e = expert(SLOTS - 1)
            pe.wait_ge(eo_done, SLOTS - 1)
            second_layer(SLOTS - 1, e)

        @block.vector
        def _(eng):
            chain = {"base": 0, "n": 0}

            def link(ins):
                chain["n"] += 1
                ins.then_inc(dve, 1)
                eng.wait_ge(dve, chain["base"] + chain["n"])

            def merge_stats(st, mean, tmp):
                eng.tensor_tensor(tmp[0], st[:, :, 1], st[:, :, 4], ALU.subtract)
                eng.tensor_tensor(tmp[1], st[:, :, 2], st[:, :, 5], ALU.add)
                link(eng.tensor_tensor(tmp[2], st[:, :, 1], st[:, :, 4], ALU.add))
                eng.tensor_scalar(mean, tmp[2], -0.5, None, ALU.mult)
                link(eng.tensor_tensor(tmp[0], tmp[0], tmp[0], ALU.mult))
                link(eng.scalar_tensor_tensor(out=tmp[1], in0=tmp[0], scalar=P / 4.0, in1=tmp[1], op0=ALU.mult, op1=ALU.add))

            def x_low(n):
                eng.wait_ge(xT_hi_done, n + 1)
                eng.tensor_tensor(xT_lo[:, :, :].rearrange("p b t -> p (b t)"), bankA[:, 0:B * P],
                                  xT_hi[:, :, :].rearrange("p b t -> p (b t)").bitcast(F32), ALU.subtract).then_inc(xT_lo_done, 1)

            def rotate(n, i):
                eng.wait_ge(qk_mm, 4 * n + i + 1)
                src = ring[i][:, :].rearrange("p (h d) -> p h d", h=H)
                cos = cos_t[:, ds(n, 1), :].broadcast_to([P, H, D])
                eng.tensor_tensor(rot[:, i, :].rearrange("p (h d) -> p h d", h=H), src, cos, ALU.mult)
                if i >= 2:
                    eng.wait_ge(rot_add, 4 * n + i - 1)
                swapped = ring[i][:, :].rearrange("p (h s d) -> p h s d", h=H, s=2)[:, :, ::-1, :]
                sin = sin_t[:, ds(n, 1), :].rearrange("p a (s d) -> p a s d", s=2).broadcast_to([P, H, 2, D // 2])
                eng.tensor_tensor(rot_sin[:, i % 2, :].rearrange("p (h s d) -> p h s d", h=H, s=2), swapped, sin,
                                  ALU.mult).then_inc(rot_mul, 1)

            SC = [[bankB, bankC], [bankD, bankA]]

            def head_stats(n, b):
                eng.wait_ge(u_mm, 2 * n + b + 1)
                for h in range(H):
                    ins = eng.bn_stats(st_u[:, b, h, :], bankU[b][h % 2][:, (h // 2) * V:(h // 2 + 1) * V])
                link(ins)
                merge_stats(st_u[:, b, :, :], mean_u[:, b, :], tmp_u)
                eng.scalar_tensor_tensor(out=ve_u[:, b, :], in0=tmp_u[1], scalar=1.0 / V, in1=cst[:, C_EPS],
                                         op0=ALU.mult, op1=ALU.add).then_inc(u_var, 1)

            def state_add(n, b, has_prev):
                eng.wait_ge(st_mm, 2 * n + b + 1)
                bank = [bankC, bankD][b]
                if has_prev:
                    eng.wait_ge(decayed, 2 * n - 2 + b + 1)
                    ins = eng.tensor_tensor(state[:, b, :], bank[:, :], state[:, b, :], ALU.add)
                else:
                    ins = eng.tensor_copy(state[:, b, :], bank[:, :])
                ins.then_inc(st_done, 1)

            def per_token(ap, n):
                return ap.unsqueeze(2).broadcast_to([P, B, n])

            def place_tokens(n):
                eng.wait_ge(rank_mm, n)
                eng.tensor_tensor(placed, bankA[:, 256:256 + B * E].rearrange("p (b e) -> p b e", b=B), chosen,
                                  ALU.mult).then_inc(rank_read, 1)
                eng.wait_ge(rank_read, n)
                link(eng.tensor_reduce(rank, placed, AX.X, ALU.add))
                link(eng.tensor_copy(rank_i[:, 0:2], rank))
                eng.tensor_scalar(rank_i[:, 2:4], rank_i[:, 0:2], 7, None, ALU.logical_shift_right)
                link(eng.tensor_scalar(rank_i[:, 4:6], rank_i[:, 0:2], P - 1, None, ALU.bitwise_and))
                eng.tensor_tensor(placed, chosen, per_token(cst[:, C_TOK][:, ds((n - 1) * B, B)], E), ALU.mult)
                link(eng.tensor_copy(route[:, 6:10], rank_i[:, 2:6]))
                link(eng.tensor_tensor(same_tile, cst[:, C_IOTA][:, 0:QT].unsqueeze(1).broadcast_to([P, B, QT]),
                                       per_token(tile_f, QT), ALU.is_equal))
                eng.tensor_tensor(one_row[:, :, :], cst[:, C_IOTA].unsqueeze(1).broadcast_to([P, B, P]), per_token(row_f, P), ALU.is_equal)
                eng.tensor_tensor(one_tile[:, :, :, :], placed.unsqueeze(3).broadcast_to([P, B, E, QT]),
                                  same_tile.unsqueeze(2).broadcast_to([P, B, E, QT]), ALU.mult).then_inc(one_done, 1)

            def add_tokens(n, turned=True):
                eng.wait_ge(ids_mm, n)
                if turned:
                    eng.wait_ge(z2T_done, n)
                eng.tensor_tensor(ids[:, :], ids[:, :], bankA[:, 256:256 + E * QT], ALU.add).then_inc(ids_add, 1)

            def choose(n):
                eng.wait_ge(lg_done, n + 1)
                link(eng.tensor_tensor(before[:, 0, :], before[:, 1, :], chosen[:, 1, :], ALU.add))
                link(eng.tensor_reduce(best, logit[:, :, :], AX.X, ALU.max))
                link(eng.tensor_tensor(eq, logit[:, :, :], per_token(best, E), ALU.is_ge))
                link(eng.tensor_tensor(eq, eq, cst[:, C_FIRST].unsqueeze(1).broadcast_to([P, B, E]), ALU.mult))
                link(eng.tensor_reduce(first, eq, AX.X, ALU.max))
                link(eng.tensor_tensor(chosen, eq, per_token(first, E), ALU.is_equal))
                eng.tensor_tensor(before[:, 1, :], before[:, 0, :], chosen[:, 0, :], ALU.add).then_inc(chosen_done, 1)
                eng.wait_ge(chosen_done, n + 1)

            def step(n, has_cur, has_prev, has_next):
                if has_cur:
                    if has_prev:
                        eng.wait_ge(st_mm, 2 * n)
                    for i in range(4):
                        rotate(n, i)
                if has_next:
                    x_low(n + 1)
                if has_prev:
                    place_tokens(n)
                if has_cur:
                    for b in range(B):
                        for par in range(2):
                            eng.wait_ge(sc_mm, 4 * n + 2 * b + par + 1)
                            eng.tensor_tensor(prob[:, b, par, :], SC[b][par][:, :], mask_t[:, par, :], ALU.mult).then_inc(sc_done, 1)
                    eng.wait_ge(w1_hi_done, n + 1)
                    eng.tensor_tensor(w1_lo[:, ds(n * F, F)], w1_stage[:, :], w1_hi[:, ds(n * F, F)].bitcast(F32),
                                      ALU.subtract).then_inc(w1_lo_done, 1)
                if has_prev:
                    eng.wait_ge(wo_mm, n)
                    eng.tensor_tensor(x2[:, :, :], x_all[:, :, ds(n - 1, 1), :].rearrange("p b a d -> p b (a d)"),
                                      bankB[:, 0:B * HID].rearrange("p (b d) -> p b d", b=B), ALU.add).then_inc(x2_done, 1)
                    eng.wait_ge(x2_done, n)
                    for b in range(B):
                        ins = eng.bn_stats(st_z[:, b, :], x2[:, b, :])
                    link(ins)
                    merge_stats(st_z, mean_z, tmp_z)
                    eng.tensor_scalar(var_z, tmp_z[1], 1.0 / P, None, ALU.mult)
                    eng.tensor_scalar(tmp_z[2], tmp_z[1], 1.0 / P, EPS, ALU.mult, ALU.add).then_inc(z_var, 1)
                    eng.wait_ge(z_rstd, 2 * n - 1)
                    for b in range(B):
                        ins = eng.tensor_scalar(z2[:, b, :], x2[:, b, :], mean_z[:, b:b + 1], rs_z[:, b:b + 1], ALU.add, ALU.mult)
                    ins.then_inc(z2_done, 1)
                    eng.wait_ge(z2_done, n)
                    eng.wait_ge(z_rstd, 2 * n)
                    for b in range(B):
                        ins = eng.tensor_scalar(rows[:, b, HID:2 * HID], z2[:, b, :], rs2_z[:, b:b + 1], None, ALU.mult)
                    ins.then_inc(rn_done, 1)
                if has_cur:
                    head_stats(n, 0)
                    head_stats(n, 1)
                if has_prev:
                    add_tokens(n)
                if has_next:
                    state_add(n, 0, has_prev)
                    state_add(n, 1, has_prev)
                if has_prev:
                    choose(n)
                    eng.wait_ge(pay_out, 16 * n)

            eng.memset(route[:, :], 0.0).then_inc(chosen_done, 1)
            eng.memset(eps_x, EPS)
            eng.memset(ids[:, :], 0.0).then_inc(ids_add, 1)
            eng.wait_ge(x_in_sem, 16)
            for b in range(B):
                for n in range(NC):
                    ins = eng.bn_stats(st_x[:, b * NC + n, :], x_all[:, b, n, :])
            link(ins)
            merge_stats(st_x[:, :, :], mean_x, tmp_x)
            eng.tensor_scalar(ve_x, tmp_x[1], 1.0 / P, EPS, ALU.mult, ALU.add).then_inc(x_var, 1)
            for i in range(3):
                eng.wait_ge(w_hi_done, i + 1)
                s = slice(1024 * i, 1024 * i + 1024)
                eng.tensor_tensor(w_lo[:, s], w_raw[:, s], w_hi[:, s].bitcast(F32), ALU.subtract).then_inc(w_lo_done, 1)
                if i == 0:
                    x_low(0)
            eng.wait_ge(c_in[0], 16)
            eng.wait_ge(c_in[1], 16)
            step(0, True, False, True)
            links = 5 + 4 + 2 * 4 + 6
            base = chain["n"]
            with eng.Fori(1, NC - 1) as n:
                chain.update(base=(n - 1) * links + base, n=0)
                step(n, True, True, True)
                assert chain["n"] == links, chain["n"]
            chain.update(base=(NC - 2) * links + base, n=0)
            step(NC - 1, True, True, False)
            step(NC, False, True, False)

            place_tokens(NC + 1)
            link(eng.tensor_tensor(over, bankC[:, 0:E].unsqueeze(2).broadcast_to([P, E, QT]),
                                   cst[:, C_STEP].unsqueeze(1).broadcast_to([P, E, QT]), ALU.is_gt))
            link(eng.tensor_reduce(ntile, over, AX.X, ALU.add))
            link(eng.tensor_tensor_scan(tile_end, ntile, zero8, 0.0, ALU.add, ALU.add))
            link(eng.tensor_tensor(below, tile_end[0:1, :].unsqueeze(1).broadcast_to([1, SLOTW, E]),
                                   cst[0:1, C_SLOT].unsqueeze(2).broadcast_to([1, SLOTW, E]), ALU.is_le))
            link(eng.tensor_reduce(passed, below, AX.X, ALU.add))
            eng.tensor_scalar(expert_i[:, :], passed, float(E - 1), None, ALU.min)
            link(eng.tensor_tensor(below, below, ntile[0:1, :].unsqueeze(1).broadcast_to([1, SLOTW, E]), ALU.mult))
            link(eng.tensor_reduce(used, below, AX.X, ALU.add))
            link(eng.tensor_tensor(used, cst[0:1, C_SLOT], used, ALU.subtract))
            eng.scalar_tensor_tensor(out=col_i[:, :], in0=passed, scalar=float(QT), in1=used, op0=ALU.mult,
                                     op1=ALU.add).then_inc(plan_done, 1)
            add_tokens(NC + 1, turned=False)
            eng.wait_ge(ids_add, NC + 2)
            link(eng.tensor_scalar(empty, ids[:, :], 0.0, float(PAD_ROW), ALU.is_equal, ALU.mult))
            eng.tensor_scalar(table[:, 0:E * QT, 0], ids[:, :], -1.0, 0.0, ALU.add, ALU.max)
            eng.scalar_tensor_tensor(out=table[:, 0:E * QT, 1], in0=ids[:, :], scalar=-1.0, in1=empty, op0=ALU.add,
                                     op1=ALU.add).then_inc(table_done, 1)

            eng.wait_ge(plan_done, 1)
            for s in b_in:
                eng.wait_ge(s, 16)

            def expert(k):
                return eng.value_load(expert_i[0:1, ds(k, 1)], min_val=0, max_val=E - 1)

            def take_rows(k, j, turn, e):
                if not (isinstance(k, int) and k == 0):
                    eng.wait_ge(ex_lo_done, k)
                eng.wait_ge(ezT_mm, k + 1)
                eng.tensor_scalar(exT, bankA[:, 0:P], lng[:, ds(e, 1)], lnb[:, ds(e, 1)], ALU.mult, ALU.add).then_inc(exT_done, 1)
                eng.wait_ge(e_in[j], 16 * (turn + 1))
                eng.tensor_tensor(resid[:, j, :], erow[:, j, 0:HID], b2_rep[:, ds(e * HID, HID)], ALU.add).then_inc(resid_done, 1)

            def rows_low(k, j):
                eng.wait_ge(ex_hi_done, k + 1)
                eng.tensor_tensor(ex_lo[:, j % 2, :], exT, ex_hi[:, j % 2, :].bitcast(F32), ALU.subtract).then_inc(ex_lo_done, 1)

            def finish(k, j):
                eng.wait_ge(y_mm, k + 1)
                eng.wait_ge(resid_done, k + 1)
                eng.tensor_tensor(eout[:, j, :], bankU[1][0][:, 0:HID], resid[:, j, :], ALU.add).then_inc(eo_done, 1)

            def tile(k, j, turn, has_prev, has_next2, stored=None):
                e = expert(k)
                e2 = expert(k + 2) if has_next2 else None
                eng.wait_ge(h_mm, k + 1)
                eng.tensor_tensor(hid, bankU[0][0][:, :], b1_rep[:, ds(e * F, F)], ALU.add).then_inc(h_done, 1)
                if has_next2:
                    take_rows(k + 2, (j + 2) % RING, turn + (j + 2) // RING, e2)
                if stored is not None and j > 0:
                    eng.wait_ge(e_out[j - 1], stored)
                if stored is not None and j == RING - 1:
                    eng.wait_ge(e_out[j], stored)
                if has_prev:
                    finish(k - 1, (j - 1) % RING)
                if has_next2:
                    rows_low(k + 2, j)

            for j in range(2):
                take_rows(j, j, 0, expert(j))
                rows_low(j, j)
            for j in range(RING):
                tile(j, j, 0, j > 0, True)
            with eng.Fori(1, (SLOTS - 3) // RING) as m:
                for j in range(RING):
                    tile(m * RING + j, j, m, True, True, 16 * m)
            for j in range(3):
                tile(SLOTS - 3 + j, j, SLOTS // RING, True, j < 1, 16 * (SLOTS // RING))
            eng.wait_ge(e_out[2], 16 * (SLOTS // RING))
            finish(SLOTS - 1, (SLOTS - 1) % RING)


def kernel(L0_attn_x, L0_attn_Wq, L0_attn_Wk, L0_attn_Wv, L0_attn_Wg, L0_attn_Wo, L0_attn_gn_weight, L0_attn_gn_bias,
           L0_ffn_centroids, L0_ffn_ln_g, L0_ffn_ln_b, L0_ffn_W1, L0_ffn_b1, L0_ffn_W2, L0_ffn_b2):
    import concourse.bacc as bacc
    from concourse.bass_utils import run_bass_kernel_spmd

    def a(v):
        return np.asarray(v)

    c = np.ascontiguousarray
    ins = {
        "x": c(a(L0_attn_x)),
        "wqkvg": c(np.concatenate([a(w) for w in (L0_attn_Wg, L0_attn_Wq, L0_attn_Wk, L0_attn_Wv)], 0).T),
        "wo": c(a(L0_attn_Wo).reshape(HID, H, V).transpose(2, 1, 0)),
        "gn": c(np.stack([a(L0_attn_gn_weight), a(L0_attn_gn_bias)]).reshape(2, H, V).transpose(2, 0, 1)),
        "cen": c(a(L0_ffn_centroids).T),
        "lng": c(a(L0_ffn_ln_g).T),
        "lnb": c(a(L0_ffn_ln_b).T),
        "w1": c(a(L0_ffn_W1).transpose(1, 0, 2)),
        "b1": c(a(L0_ffn_b1).reshape(-1)),
        "w2": c(a(L0_ffn_W2).reshape(E, FC, P, HID).transpose(2, 0, 1, 3)),
        "b2": c(a(L0_ffn_b2).reshape(-1)),
        "constants": constants(),
    }
    nc = bacc.Bacc("TRN2", target_bir_lowering=False, num_devices=1)
    args = [nc.dram_tensor(f"in_{n}", v.shape, mybir.dt.from_np(v.dtype), kind="ExternalInput").ap() for n, v in ins.items()]
    out = nc.dram_tensor("out", (B, T, HID), F32, kind="ExternalOutput").ap()
    preln_retention_moe_kernel(nc, *args, out)
    r = run_bass_kernel_spmd(nc, [{f"in_{n}": v for n, v in ins.items()}], core_ids=[0])
    return r.results[0]["out"]
```

```python
from contextlib import ExitStack

import numpy as np

import concourse.bass as bass
from concourse import mybir

F32 = mybir.dt.float32
F32R = mybir.dt.float32r
I32 = mybir.dt.int32
U32 = mybir.dt.uint32
ALU = mybir.AluOpType
ACT = mybir.ActivationFunctionType
AX = mybir.AxisListType
ds = bass.ds

P = 128
B, T, HID = 2, 1024, 128
H, D, V = 8, 64, 128
NC = T // P
HP = H // 2
E, F = 8, 512
FC = F // P
EPS = 1e-5
NTOK = B * T
NT = NTOK // P
SLOTS = NT + E - 1
SLOTW = SLOTS + 1
QT = NT
RING = 4
LEAD = RING + 1
LAG = LEAD + 1

_at = 0


def _col(n):
    global _at
    _at += n
    return slice(_at - n, _at)


C_ID = _col(P)
C_COS = _col(NC * D)
C_SIN = _col(NC * D)
C_GV = _col(H)
C_EPS = _col(H)
C_GCV = _col(HP * V)
C_MASK = _col(H * P)
C_PART = _col(1)
C_PAD = _col(1)
C_TRI = _col(P)
C_IOTA = _col(P)
C_SLOT = _col(SLOTW)
C_FIRST = _col(E)
C_STEP = _col(NT)
C_TOK = _col(NT)
C_ONES = _col(P)
C_ALL = _at


def constants():
    c = np.zeros((P, C_ALL), np.float32)
    i = np.arange(P)
    c[:, C_ID] = np.eye(P)
    inv = (np.float32(1.0) / np.float32(10000.0) ** (np.arange(0, D, 2, dtype=np.float32) / np.float32(D))).astype(np.float32)
    ang = np.arange(T, dtype=np.float32)[:, None] * inv[None, :]
    cos = np.concatenate([np.cos(ang), np.cos(ang)], 1)
    sin = np.concatenate([-np.sin(ang), np.sin(ang)], 1)
    c[:, C_COS] = cos.reshape(NC, P, D).transpose(1, 0, 2).reshape(P, -1)
    c[:, C_SIN] = sin.reshape(NC, P, D).transpose(1, 0, 2).reshape(P, -1)
    gamma = 1.0 - 2.0 ** (-5.0 - np.arange(H, dtype=np.float64))
    c[:, C_GV] = gamma[None, :] ** (P - i)[:, None]
    c[:, C_EPS] = D * EPS * gamma[None, :] ** (-2.0 * i)[:, None]
    for half in range(2):
        c[half * D:(half + 1) * D, C_GCV] = np.repeat(gamma[half::2] ** P, V)
    causal = (i[None, :] >= i[:, None]).astype(np.float64)
    order = [2 * p + half for half in range(2) for p in range(HP)]
    c[:, C_MASK] = (causal[:, None, :] * gamma[order][None, :, None] ** -i[:, None, None].astype(np.float64)).reshape(P, -1)
    c[:, C_TRI] = i[:, None] < i[None, :]
    c[:, C_IOTA] = i
    c[:, C_PART] = i[:, None]
    c[:, C_PAD] = NTOK + 1 + i[:, None]
    c[:, C_SLOT] = np.arange(SLOTW)
    c[:, C_FIRST] = E - np.arange(E)
    c[:, C_STEP] = P * np.arange(NT)
    tok = (np.arange(B)[None, None, :] * T + np.arange(NC)[None, :, None] * P + i[:, None, None]) + 1
    c[:, C_TOK] = tok.reshape(P, NT)
    c[:, C_ONES] = 1.0
    return c


def preln_retention_moe_kernel(nc, x_in, wqkvg_in, wo_in, gn_in, cen_in, lng_in, lnb_in,
                               w1_in, b1_in, w2_in, b2_in, const_in, out):
    ctx = ExitStack()
    with ctx:
        def sb(name, shape, dt=F32):
            return ctx.enter_context(nc.sbuf_tensor(name, shape, dt))

        def sem(name):
            return ctx.enter_context(nc.semaphore(name))

        payload = nc.dram_tensor("payload", (NTOK, 2 * HID), F32, kind="Internal").ap()

        cst = sb("cst", [P, C_ALL])
        x_all = sb("x_all", [P, B, NC, HID])
        w_raw = sb("w_raw", [P, 3072])
        w_hi = sb("w_hi", [P, 3072], F32R)
        w_lo = sb("w_lo", [P, 3072], F32R)
        wo = sb("wo", [P, H, HID])
        gn = sb("gn", [P, 2, H])
        cen = sb("cen", [P, E])
        lng = sb("lng", [P, E])
        lnb = sb("lnb", [P, E])
        w1 = sb("w1", [P, E * F])
        w2 = sb("w2", [P, E, FC, HID])
        b2_rep = sb("b2_rep", [P, E * HID])
        b1 = sb("b1", [P, E * FC])

        xn = sb("xn", [P, B, HID])
        xT_hi = sb("xT_hi", [P, B, P], F32R)
        xT_lo = sb("xT_lo", [P, B, P], F32R)
        rot = sb("rot", [P, 4, 512])
        rot_sin = sb("rot_sin", [P, 2, 512])
        kg = sb("kg", [P, B, 512])
        v_sb = sb("v_sb", [P, B, H * V])
        qkT = sb("qkT", [P, 4, 512])
        prob = sb("prob", [P, B, 2, 512])
        state = sb("state", [P, B, HP * V])
        z = sb("z", [P, B, H * V])
        sg = sb("sg", [P, 2, H, B * P])
        yT = sb("yT", [P, H, B * P])
        x2 = sb("x2", [P, B, HID])
        z2 = sb("z2", [P, B, HID])
        z2T = sb("z2T", [P, B, P])
        rows = sb("rows", [P, B, 2 * HID])
        logit = sb("logit", [P, B, E])
        half_row = sb("half_row", [P, NT])
        small = sb("small", [P, 256])

        st_x = sb("st_x", [P, NT, 6])
        mean_x, ve_x, rs_x, nb_x = [small[:, 16 * k:16 * k + 16] for k in range(4)]
        tmp_x = [small[:, 64 + 16 * k:80 + 16 * k] for k in range(3)]
        st_z = small[:, 112:124].rearrange("p (g s) -> p g s", g=B)
        var_z, mean_z, rs_z, rs2_z, pool_z, nb_z = [small[:, 124 + 2 * k:126 + 2 * k] for k in range(6)]
        tmp_z = [small[:, 136 + 2 * k:138 + 2 * k] for k in range(3)]
        eps_x = small[:, 142:158]
        st_u = sb("st_u", [P, B, H, 6])
        ve_u, rs_u, mean_u, nb_u = [small[:, 158 + 16 * k:174 + 16 * k].rearrange("p (b h) -> p b h", b=B) for k in range(4)]
        tmp_u = [small[:, 222 + 8 * k:230 + 8 * k] for k in range(3)]

        bankA, bankB, bankC, bankD = [ctx.enter_context(nc.psum_tensor(f"bank{c}", [P, 512], F32)) for c in "ABCD"]
        ring = [bankA, bankD, bankB, bankC]
        bankU = [[ctx.enter_context(nc.psum_tensor(f"bankU{b}{par}", [P, 512], F32)) for par in range(2)] for b in range(B)]

        route = sb("route", [P, 128])
        best, first, rank, tile_f, row_f = [route[:, 2 * k:2 * k + 2] for k in range(5)]
        eq, chosen, before, placed = [route[:, 16 + 16 * k:32 + 16 * k].rearrange("p (b e) -> p b e", b=B) for k in range(4)]
        same_tile = sb("same_tile", [P, B, QT])[:, :, :]
        ntile, tile_end, zero8, spare = [route[:, 80 + 8 * k:88 + 8 * k] for k in range(4)]
        rank_i = sb("rank_i", [P, 6], I32)
        one_row = sb("one_row", [P, B, P])
        one_tile = sb("one_tile", [P, B, E, QT])
        ids = sb("ids", [E * QT, P])
        plan = rot_sin[:, :, :].rearrange("p a n -> p (a n)")
        over = plan[:, 0:128].rearrange("p (e j) -> p e j", e=E)
        below = plan[:, 128:320].rearrange("p (k e) -> p k e", e=E)
        below2 = plan[:, 320:512].rearrange("p (k e) -> p k e", e=E)
        passed, col, empty = [plan[:, 512 + SLOTW * k:512 + SLOTW * (k + 1)] for k in range(3)]
        slot_col = sb("slot_col", [P, SLOTW])
        table = sb("table", [P, SLOTW + LAG, 2], U32)
        at = sb("at", [P, RING, 2], U32)
        zero_u = sb("zero_u", [P, 2], U32)
        expert_i = sb("expert_i", [1, SLOTW], I32)

        sgf = sg[:, :, :, :].rearrange("p a h n -> p (a h n)")
        erow = sgf[:, 0:1024].rearrange("p (r n) -> p r n", r=RING)
        eout = sgf[:, 1024:1536].rearrange("p (r n) -> p r n", r=RING)
        resid = sgf[:, 1536:2048].rearrange("p (r n) -> p r n", r=RING)
        exT = sgf[:, 2048:2048 + 2 * P].rearrange("p (a t) -> p a t", a=2)
        hidT = sgf[:, 2560:3584].rearrange("p (a c t) -> p a c t", a=2, c=FC)
        w1_cur = sb("w1_cur", [P, 2, F])
        w2_cur = sb("w2_cur", [P, RING, F])
        b1_cur = sb("b1_cur", [P, RING, FC])

        ident = cst[:, C_ID]
        cos_t = cst[:, C_COS].rearrange("p (n d) -> p n d", d=D)
        sin_t = cst[:, C_SIN].rearrange("p (n d) -> p n d", d=D)
        mask_t = cst[:, C_MASK].rearrange("p (a n) -> p a n", a=2)

        x_in_sem = [sem(f"x_in_sem{i}") for i in range(2)]
        id_in = sem("id_in")
        c_in = [sem(f"c_in{i}") for i in range(2)]
        w_in = [sem(f"w_in{i}") for i in range(3)]
        small_in = sem("small_in")
        wo_in_sem = sem("wo_in_sem")
        w1_in_sem = sem("w1_in_sem")
        w2_in_sem = sem("w2_in_sem")
        b_in = [sem("b1_in_sem"), sem("b2_in_sem")]
        w_hi_done, w_lo_done = sem("w_hi_done"), sem("w_lo_done")
        x_var, x_rstd, x_nb = sem("x_var"), sem("x_rstd"), sem("x_nb")
        xn_done = sem("xn_done")
        xT_mm, xT_hi_done, xT_lo_done = sem("xT_mm"), sem("xT_hi_done"), sem("xT_lo_done")
        g_mm, sg_done = sem("g_mm"), sem("sg_done")
        qk_mm, rot_mul, rot_add = sem("qk_mm"), sem("rot_mul"), sem("rot_add")
        v_mm, v_done = sem("v_mm"), sem("v_done")
        qkT_mm, qkT_done = sem("qkT_mm"), sem("qkT_done")
        sc_mm, sc_done = sem("sc_mm"), sem("sc_done")
        u_mm, u_var, u_rstd, z_done = sem("u_mm"), sem("u_var"), sem("u_rstd"), sem("z_done")
        kg_done, decayed, st_mm, st_done = sem("kg_done"), sem("decayed"), sem("st_mm"), sem("st_done")
        zT_mm, za_done, y_done, y_dve = sem("zT_mm"), sem("za_done"), sem("y_done"), sem("y_dve")
        wo_mm, x2_done = sem("wo_mm"), sem("x2_done")
        z_var, z_rstd, z_nb, z2_done, rn_done, rs_done = (sem(n) for n in ("z_var", "z_rstd", "z_nb", "z2_done", "rn_done", "rs_done"))
        z2T_mm, z2T_done, lg_mm, lg_done = sem("z2T_mm"), sem("z2T_done"), sem("lg_mm"), sem("lg_done")
        pay_out = sem("pay_out")
        dve = sem("dve_chain")
        pool_init, pool_chain = sem("pool_init"), sem("pool_chain")
        chosen_done, rank_mm, rank_read, one_done, ids_mm, ids_add = (
            sem(n) for n in ("chosen_done", "rank_mm", "rank_read", "one_done", "ids_mm", "ids_add"))
        columns_done, plan_done, table_done = sem("columns_done"), sem("plan_done"), sem("table_done")
        row_placed = sem("row_placed")
        e_in = [sem(f"e_in{i}") for i in range(RING)]
        e_out = [sem(f"e_out{i}") for i in range(RING)]
        totals_mm, slots_mm = sem("totals_mm"), sem("slots_mm")
        ezT_mm, exT_done, w1_done, w2_done, h_mm, hid_part, hid_done = (
            sem(n) for n in ("ezT_mm", "exT_done", "w1_done", "w2_done", "h_mm", "hid_part", "hid_done"))
        y_mm, eo_done, resid_done = (sem(n) for n in ("y_mm", "eo_done", "resid_done"))

        block = ctx.enter_context(nc.Block())

        @block.sync
        def _(sp):
            x_rows = x_in.rearrange("b (n p) d -> p b n d", p=P)
            for b in range(B):
                sp.dma_start(x_all[:, b, 0:2, :], x_rows[:, b, 0:2, :]).then_inc(x_in_sem[0], 16)
            sp.dma_start(cst[:, C_ID], const_in[:, C_ID]).then_inc(id_in, 16)
            for i in range(3):
                sp.dma_start(w_raw[:, 1024 * i:1024 * i + 1024], wqkvg_in[:, 1024 * i:1024 * i + 1024]).then_inc(w_in[i], 16)
            sp.dma_start(cst[:, P:C_GCV.start], const_in[:, P:C_GCV.start]).then_inc(c_in[0], 16)
            for b in range(B):
                sp.dma_start(x_all[:, b, 2:NC, :], x_rows[:, b, 2:NC, :]).then_inc(x_in_sem[1], 16)
            sp.dma_start(cst[:, C_GCV.start:C_ALL], const_in[:, C_GCV.start:C_ALL]).then_inc(c_in[1], 16)
            sp.dma_start(gn[:, :, :], gn_in).then_inc(small_in, 16)
            sp.dma_start(cen[:, :], cen_in).then_inc(small_in, 16)
            sp.dma_start(lng[:, :], lng_in).then_inc(small_in, 16)
            sp.dma_start(lnb[:, :], lnb_in).then_inc(small_in, 16)
            sp.dma_start(wo[:, :, :], wo_in).then_inc(wo_in_sem, 16)
            sp.dma_start(w1[:, :], w1_in).then_inc(w1_in_sem, 16)
            sp.dma_start(w2[:, :, :, :], w2_in).then_inc(w2_in_sem, 16)
            sp.dma_start(b1[:, :], b1_in).then_inc(b_in[0], 16)
            sp.dma_start(b2_rep[:, :], b2_in.partition_broadcast(P)).then_inc(b_in[1], 16)

            def store_rows(n):
                sp.wait_ge(rn_done, n)
                sp.wait_ge(rs_done, n)
                sp.dma_start(payload.rearrange("(b n p) c -> p b n c", b=B, p=P)[:, :, ds(n - 1, 1), :]
                             .rearrange("p b a c -> p b (a c)"), rows[:, :, :]).then_inc(pay_out, 16)

            with sp.Fori(1, NC + 1) as n:
                store_rows(n)

        @block.gpsimd
        def _(pool):
            chain = {"base": 0, "n": 0}

            def link(ins):
                chain["n"] += 1
                ins.then_inc(pool_chain, 1)
                pool.wait_ge(pool_chain, chain["base"] + chain["n"])

            pool.memset(half_row[:, :], -0.5).then_inc(pool_init, 1)
            pool.memset(zero_u[:, :], 0).then_inc(pool_init, 1)
            pool.memset(table[:, :, :], 0).then_inc(pool_init, 1)
            pool.wait_ge(pool_init, 3)

            def rstd(out_ap, in_ap):
                return pool.tensor_tensor(out_ap, in_ap, half_row[:, 0:in_ap.shape[1]], ALU.pow)

            def rstd_heads(n, b):
                pool.wait_ge(u_var, 2 * n + b + 1)
                link(rstd(rs_u[:, b, :], ve_u[:, b, :]))
                pool.tensor_tensor(nb_u[:, b, :], mean_u[:, b, :], rs_u[:, b, :], ALU.mult).then_inc(u_rstd, 1)

            def decay_state(n, b):
                pool.wait_ge(u_mm, 2 * n + b + 1)
                pool.tensor_tensor(state[:, b, :], state[:, b, :], cst[:, C_GCV], ALU.mult).then_inc(decayed, 1)

            def rotate(n, i):
                pool.wait_ge(rot_mul, 4 * n + i + 1)
                pool.tensor_tensor(rot[:, i, :], rot[:, i, :], rot_sin[:, i % 2, :], ALU.add).then_inc(rot_add, 1)

            def gate(n, j):
                pool.wait_ge(za_done, 4 * n + j + 1)
                y = yT[:, 2 * j:2 * j + 2, :].rearrange("p h n -> p (h n)")
                pool.tensor_tensor(y, y, sg[:, ds(n % 2, 1), 2 * j:2 * j + 2, :].rearrange("p a h n -> p (a h n)"),
                                   ALU.mult).then_inc(y_done, 1)

            def weigh_keys(n, b):
                pool.wait_ge(rot_add, 4 * n + 2 * b + 2)
                pool.tensor_tensor(kg[:, b, :].rearrange("p (h d) -> p h d", h=H),
                                   rot[:, 2 * b + 1, :].rearrange("p (h d) -> p h d", h=H),
                                   cst[:, C_GV].unsqueeze(2).broadcast_to([P, H, D]), ALU.mult).then_inc(kg_done, 1)

            def step(n, prev2, prev, cur, next1, next2):
                if prev:
                    gate(n - 1, 0)
                    if cur:
                        gate(n - 1, 1)
                if next1:
                    for i in range(4):
                        rotate(n + 1, i)
                if prev:
                    gate(n - 1, 2)
                    if cur:
                        gate(n - 1, 3)
                if cur:
                    rstd_heads(n, 0)
                    if prev and next1:
                        decay_state(n, 0)
                        decay_state(n, 1)
                    rstd_heads(n, 1)
                if prev:
                    pool.wait_ge(z_var, n)
                    rstd(rs_z, tmp_z[2]).then_inc(z_rstd, 1)
                    pool.wait_ge(z_rstd, 2 * n - 1)
                    link(pool.tensor_tensor(pool_z, rs_z, rs_z, ALU.mult))
                    link(pool.tensor_tensor(pool_z, pool_z, var_z, ALU.mult))
                    link(pool.tensor_tensor(pool_z, pool_z, eps_x[:, 0:B], ALU.add))
                    rstd(rs2_z, pool_z).then_inc(z_rstd, 1)
                    if prev2:
                        pool.wait_ge(pay_out, 16 * n - 16)
                    pool.wait_ge(z2_done, n)
                    pool.tensor_tensor(rows[:, :, 0:HID], x2[:, :, :], z2[:, :, :], ALU.add).then_inc(rs_done, 1)
                if next2:
                    for b in range(B):
                        pool.wait_ge(st_mm, 2 * n + b + 1)
                        weigh_keys(n + 1, b)

            def rstd_x(i, c):
                pool.wait_ge(x_var, i + 1)
                link(rstd(rs_x[:, c], ve_x[:, c]))
                pool.tensor_tensor(nb_x[:, c], mean_x[:, c], rs_x[:, c], ALU.mult).then_inc(x_nb, 1)

            rstd_x(0, slice(0, 2 * B))
            for i in range(4):
                rotate(0, i)
            for b in range(B):
                weigh_keys(0, b)
            rstd_x(1, slice(2 * B, NT))
            step(0, False, False, True, True, True)
            step(1, False, True, True, True, True)
            links = 3 + 2
            base = chain["n"]
            with pool.Fori(2, NC - 2) as n:
                chain.update(base=(n - 2) * links + base, n=0)
                step(n, True, True, True, True, True)
                assert chain["n"] == links, chain["n"]
            chain.update(base=(NC - 4) * links + base, n=0)
            step(NC - 2, True, True, True, True, False)
            step(NC - 1, True, True, True, False, False)
            step(NC, True, True, False, False, False)

            last_token = pool.to_reg(NTOK - 1)

            def place(t, slot):
                pool.tensor_tensor(at[:, slot, :], table[:, ds(t, 1), :].rearrange("p a w -> p (a w)"), zero_u[:, :],
                                   ALU.add).then_inc(row_placed, 1)

            def gather(j, slot):
                pool.indirect_dma_start(out=erow[:, j, :], out_offset=None, in_=payload,
                                        in_offset=bass.IndirectOffsetOnAxis(ap=at[:, slot, 1:2], axis=0),
                                        bounds_check=last_token, oob_is_err=False).then_inc(e_in[j], 16)

            def scatter(j):
                pool.indirect_dma_start(out=out.rearrange("b t d -> (b t) d"), in_=eout[:, j, :], in_offset=None,
                                        out_offset=bass.IndirectOffsetOnAxis(ap=at[:, (j + 1) % RING, 0:1], axis=0),
                                        bounds_check=last_token, oob_is_err=False).then_inc(e_out[j], 16)

            def tile(k, j, turn, has_prev2, has_gather):
                if has_gather:
                    pool.wait_ge(resid_done, k + 1)
                    pool.wait_ge(ezT_mm, k + 2)
                if has_prev2:
                    pool.wait_ge(eo_done, k - 1)
                if not (isinstance(turn, int) and turn == 0):
                    if j > 0:
                        pool.wait_ge(e_out[j - 1], 16 * turn)
                    if j == RING - 1:
                        pool.wait_ge(e_out[j], 16 * turn)
                pool.wait_ge(row_placed, k + LEAD)
                place(k + LEAD, j)
                if has_gather:
                    gather(j, (j - 1) % RING)
                if has_prev2:
                    scatter((j - 2) % RING)

            pool.wait_ge(table_done, 1)
            for j in range(RING):
                place(j, (j - 1) % RING)
                pool.wait_ge(row_placed, j + 1)
                if j == 0:
                    pool.wait_ge(pay_out, 16 * NC)
                gather(j, (j - 1) % RING)
            pool.wait_ge(e_in[0], 16)
            place(RING, RING - 1)
            for j in range(RING):
                tile(j, j, 0, j > 1, True)
            with pool.Fori(1, (SLOTS - 7) // RING) as m:
                for j in range(RING):
                    tile(m * RING + j, j, m, True, True)
            for k in range(SLOTS - 7, SLOTS):
                tile(k, k % RING, k // RING, True, k + 4 < SLOTS)
            pool.wait_ge(eo_done, SLOTS - 1)
            pool.wait_ge(e_out[(SLOTS - 5) % RING], 16 * len(range((SLOTS - 5) % RING, SLOTS - 4, RING)))
            pool.wait_ge(row_placed, SLOTS + LEAD)
            place(SLOTS + LEAD, SLOTS % RING)
            scatter((SLOTS - 2) % RING)
            pool.wait_ge(eo_done, SLOTS)
            pool.wait_ge(row_placed, SLOTS + LEAD + 1)
            scatter((SLOTS - 1) % RING)
            for j in range(RING):
                pool.wait_ge(e_out[j], 16 * len(range(j, SLOTS, RING)))

        @block.scalar
        def _(act):
            def normalise_x(n):
                if isinstance(n, int) and n == 0:
                    act.wait_ge(x_nb, 1)
                else:
                    act.wait_ge(xT_mm, n)
                for b in range(B):
                    a = act.activation(xn[:, b, :], x_all[:, b, ds(n, 1), :].rearrange("p a d -> p (a d)"), ACT.Identity,
                                       scale=rs_x[:, ds(n * B + b, 1)], bias=nb_x[:, ds(n * B + b, 1)])
                a.then_inc(xn_done, 1)

            def x_high(n):
                act.wait_ge(xT_mm, n + 1)
                act.activation(xT_hi[:, :, :].rearrange("p b t -> p (b t)"), bankU[0][1][:, 0:B * P], ACT.Copy).then_inc(xT_hi_done, 1)

            def normalise_heads(n, b):
                act.wait_ge(u_rstd, 2 * n + b + 1)
                for h in range(H):
                    a = act.activation(z[:, b, h * V:(h + 1) * V], bankU[b][h % 2][:, (h // 2) * V:(h // 2 + 1) * V], ACT.Identity,
                                       scale=rs_u[:, b, h:h + 1], bias=nb_u[:, b, h:h + 1])
                a.then_inc(z_done, 1)

            def open_gate(n, prev2):
                for j in range(4):
                    act.wait_ge(g_mm, 4 * n + j + 1)
                    if prev2:
                        act.wait_ge(y_done, 4 * n - 7 + j)
                    act.activation(sg[:, ds(n % 2, 1), 2 * j:2 * j + 2, :].rearrange("p a h n -> p (a h n)"),
                                   ring[j][:, :], ACT.Silu).then_inc(sg_done, 1)

            def weigh_heads(n, j):
                act.wait_ge(zT_mm, 4 * n + 1 + j)
                for h in (2 * j, 2 * j + 1):
                    a = act.activation(yT[:, h, :], bankU[j // 2][j % 2][:, (h % 2) * 256:(h % 2) * 256 + 256], ACT.Identity,
                                       scale=gn[:, 0, h:h + 1], bias=gn[:, 1, h:h + 1])
                a.then_inc(za_done, 1)

            def copy_z2(n, bank):
                act.wait_ge(z2T_mm, n + 1)
                act.activation(z2T[:, :, :].rearrange("p b t -> p (b t)"), bank[:, 0:B * P], ACT.Copy).then_inc(z2T_done, 1)

            def copy_logits(n, bank):
                act.wait_ge(lg_mm, n + 1)
                act.activation(logit[:, :, :].rearrange("p b e -> p (b e)"), bank[:, 256:256 + B * E], ACT.Copy).then_inc(lg_done, 1)

            def copy_v(n):
                for i in range(4):
                    act.wait_ge(v_mm, 4 * n + i + 1)
                    act.activation(v_sb[:, i // 2, 512 * (i % 2):512 * (i % 2) + 512], ring[i][:, :], ACT.Copy).then_inc(v_done, 1)

            def copy_qk(n):
                for i in range(4):
                    act.wait_ge(qkT_mm, 4 * n + i + 1)
                    act.activation(qkT[:, i, :], ring[i][:, :], ACT.Copy).then_inc(qkT_done, 1)

            def step(n, prev2, prev, cur, next1, next2):
                if prev:
                    for j in range(4):
                        weigh_heads(n - 1, j)
                        if j == 1 and not cur:
                            copy_logits(n - 2, bankB)
                if next1:
                    open_gate(n + 1, prev)
                if next2:
                    normalise_x(n + 2)
                if cur:
                    normalise_heads(n, 0)
                if next1:
                    copy_v(n + 1)
                if prev and next1:
                    copy_z2(n - 1, bankU[0][0])
                if next2:
                    x_high(n + 2)
                if next1:
                    copy_qk(n + 1)
                if prev and next1:
                    copy_logits(n - 1, bankU[0][0])
                if cur:
                    normalise_heads(n, 1)
                if not next1:
                    copy_z2(n - 1, bankB)
                if not cur:
                    copy_logits(n - 1, bankB)

            for i in range(3):
                act.wait_ge(w_in[i], 16)
                act.activation(w_hi[:, 1024 * i:1024 * i + 1024], w_raw[:, 1024 * i:1024 * i + 1024], ACT.Copy).then_inc(w_hi_done, 1)
                if i == 0:
                    normalise_x(0)
                elif i == 1:
                    x_high(0)
            normalise_x(1)
            open_gate(0, False)
            copy_v(0)
            x_high(1)
            copy_qk(0)
            act.wait_ge(x_nb, 2)
            act.wait_ge(small_in, 64)
            step(0, False, False, True, True, True)
            step(1, False, True, True, True, True)
            with act.Fori(2, NC - 2) as n:
                step(n, True, True, True, True, True)
            step(NC - 2, True, True, True, True, False)
            step(NC - 1, True, True, True, False, False)
            step(NC, True, True, False, False, False)

            act.wait_ge(plan_done, 1)
            for w in (w1_in_sem, w2_in_sem, b_in[0]):
                act.wait_ge(w, 16)

            def fetch_weights(k, j):
                e = act.value_load(expert_i[0:1, ds(k, 1)], min_val=0, max_val=E - 1)
                act.activation(w1_cur[:, j % 2, :], w1[:, ds(e * F, F)], ACT.Copy)
                act.activation(b1_cur[:, j, :], b1[:, ds(e * FC, FC)], ACT.Copy).then_inc(w1_done, 1)
                act.activation(w2_cur[:, j, :], w2[:, :, :, :].rearrange("p e c d -> p (e c d)")[:, ds(e * F, F)],
                               ACT.Copy).then_inc(w2_done, 1)

            def tile(k, j, has_prev2):
                if has_prev2:
                    act.wait_ge(y_mm, k - 1)
                act.wait_ge(h_mm, k + 1)
                fetch_weights(k + 2, (j + 2) % RING)

            fetch_weights(0, 0)
            fetch_weights(1, 1)
            for j in range(RING):
                tile(j, j, j >= 2)
            with act.Fori(1, (SLOTS - 3) // RING) as m:
                for j in range(RING):
                    tile(m * RING + j, j, True)
            tile(SLOTS - 3, 0, True)

        @block.tensor
        def _(pe):
            def split3(out_ap, l_hi, l_lo, r_hi, r_lo):
                pe.matmul(out_ap, l_hi, r_hi, start=True, stop=False)
                pe.matmul(out_ap, l_hi, r_lo, start=False, stop=False)
                return pe.matmul(out_ap, l_lo, r_hi, start=False, stop=True)

            def x_turn(n):
                pe.wait_ge(xn_done, n + 1)
                for b in range(B):
                    mm = pe.transpose(bankU[0][1][:, b * P:(b + 1) * P], xn[:, b, :], ident)
                mm.then_inc(xT_mm, 1)

            def project_qk(n, free, values):
                pe.wait_ge(xT_lo_done, n + 1)
                for i in range(4):
                    pe.wait_ge(free, values[i])
                    s = slice(1024 + 512 * (i % 2), 1536 + 512 * (i % 2))
                    split3(ring[i][:, :], xT_hi[:, i // 2, :], xT_lo[:, i // 2, :], w_hi[:, s], w_lo[:, s]).then_inc(qk_mm, 1)

            def project_g(n, prev3):
                pe.wait_ge(xT_lo_done, n + 1)
                for j in range(4):
                    if not (isinstance(n, int) and n == 0):
                        pe.wait_ge(rot_mul, 4 * n + j + 1)
                        if j == 0 and prev3:
                            pe.wait_ge(rank_read, n - 2)
                    for c in (2 * j, 2 * j + 1):
                        s = slice(c * P, (c + 1) * P)
                        mm = split3(ring[j][:, (c % 2) * 256:(c % 2) * 256 + 256], w_hi[:, s], w_lo[:, s],
                                    xT_hi[:, :, :].rearrange("p b t -> p (b t)"), xT_lo[:, :, :].rearrange("p b t -> p (b t)"))
                    mm.then_inc(g_mm, 1)

            def project_v(n, prev3, prev2, prev):
                for i in range(4):
                    if not prev:
                        pe.wait_ge(rot_mul, 4 * n + i + 1)
                    elif i == 0:
                        if prev2:
                            pe.wait_ge(x2_done, n - 1)
                        else:
                            pe.wait_ge(sg_done, 4 * n + 1)
                    elif i >= 2:
                        pe.wait_ge(st_done, 2 * n - 3 + i)
                    elif prev3:
                        pe.wait_ge(ids_add, n - 2)
                    else:
                        pe.wait_ge(sg_done, 4 * n + 2)
                    s = slice(2048 + 512 * (i % 2), 2560 + 512 * (i % 2))
                    split3(ring[i][:, :], xT_hi[:, i // 2, :], xT_lo[:, i // 2, :], w_hi[:, s], w_lo[:, s]).then_inc(v_mm, 1)

            def turn_z(n, logits_read, has_x):
                pe.wait_ge(z_done, 2 * n + 2)
                for j in range(4):
                    if j == 0 and logits_read is not None:
                        pe.wait_ge(lg_done, logits_read)
                    if j == 1 and has_x:
                        pe.wait_ge(xT_lo_done, n + 3)
                    for h in (2 * j, 2 * j + 1):
                        for b in range(B):
                            c = (h % 2) * 256 + b * P
                            mm = pe.transpose(bankU[j // 2][j % 2][:, c:c + P], z[:, b, h * V:(h + 1) * V], ident)
                    mm.then_inc(zT_mm, 1)

            def turn_qk(n):
                for i in range(4):
                    pe.wait_ge(rot_add, 4 * n + i + 1)
                    pe.wait_ge(v_done, 4 * n + i + 1)
                    for p in range(HP):
                        mm = pe.transpose(ring[i][:, p * P:(p + 1) * P], rot[:, i, p * P:(p + 1) * P], ident)
                    mm.then_inc(qkT_mm, 1)

            def rank_tokens(n, bank):
                pe.wait_ge(chosen_done, n + 1)
                o = bank[:, 0:B * E]
                pe.matmul(o, cst[:, C_TRI], chosen.rearrange("p b e -> p (b e)"), start=True, stop=False)
                pe.matmul(o, cst[:, C_ONES], before.rearrange("p b e -> p (b e)"), start=False, stop=True).then_inc(rank_mm, 1)

            def spread_tokens(n):
                pe.wait_ge(one_done, n + 1)
                for b in range(B):
                    mm = pe.matmul(bankD[:, 0:P], one_tile[:, b, :, :].rearrange("p e q -> p (e q)"), one_row[:, b, :],
                                   start=(b == 0), stop=(b == B - 1))
                mm.then_inc(ids_mm, 1)

            def scores(n, b):
                pe.wait_ge(qkT_done, 4 * n + 2 * b + 2)
                for h in range(H):
                    par, p = h % 2, h // 2
                    q = qkT[par * D:(par + 1) * D, 2 * b, p * P:(p + 1) * P]
                    k = qkT[par * D:(par + 1) * D, 2 * b + 1, p * P:(p + 1) * P]
                    mm = pe.matmul(ring[2 * b + par][:, p * P:(p + 1) * P], k, q, start=True, stop=True)
                    if h >= H - 2:
                        mm.then_inc(sc_mm, 1)

            def project_out_pair(n, j):
                if j % 2 == 0:
                    pe.wait_ge(y_done, 4 * n + j // 2 + 1)
                else:
                    pe.wait_ge(y_dve, j // 2 + 1)
                for h in (2 * j, 2 * j + 1):
                    for b in range(B):
                        mm = pe.matmul([bankC, bankU[0][0]][b][:, 0:HID], yT[:, h, b * P:(b + 1) * P], wo[:, h, :],
                                       start=(h == 0), stop=(h == H - 1))
                return mm

            def project_out(n):
                pe.wait_ge(y_done, 4 * n + 4)
                for b in range(B):
                    for h in range(H):
                        mm = pe.matmul(bankA[:, b * HID:(b + 1) * HID], yT[:, h, b * P:(b + 1) * P], wo[:, h, :],
                                       start=(h == 0), stop=(h == H - 1))
                mm.then_inc(wo_mm, 1)

            def retain(n, b, prev):
                pe.wait_ge(sc_done, 4 * n + 2 * b + 2)
                if prev:
                    pe.wait_ge(za_done, 4 * n - 2 + 2 * b)
                    pe.wait_ge(st_done, 2 * n - 1 + b)
                for p in range(HP):
                    if prev:
                        for par in range(2):
                            hs = slice(par * D, (par + 1) * D)
                            pe.matmul(bankU[b][par][:, p * V:(p + 1) * V], qkT[hs, 2 * b, p * P:(p + 1) * P],
                                      state[hs, b, p * V:(p + 1) * V], start=True, stop=False)
                    for par in range(2):
                        h = 2 * p + par
                        mm = pe.matmul(bankU[b][par][:, p * V:(p + 1) * V], prob[:, b, par, p * P:(p + 1) * P],
                                       v_sb[:, b, h * V:(h + 1) * V], start=not prev, stop=True)
                mm.then_inc(u_mm, 1)

            def update_state(n, b):
                pe.wait_ge(kg_done, 2 * n + b + 1)
                pe.wait_ge(sg_done, 4 * n + 7 + b)
                for h in range(H):
                    par, p = h % 2, h // 2
                    mm = pe.matmul([bankB, bankC][b][par * D:(par + 1) * D, p * V:(p + 1) * V],
                                   kg[:, b, h * D:(h + 1) * D], v_sb[:, b, h * V:(h + 1) * V], start=True, stop=True)
                mm.then_inc(st_mm, 1)

            def turn_z2(n, bank):
                pe.wait_ge(z2_done, n + 1)
                for b in range(B):
                    mm = pe.transpose(bank[:, b * P:(b + 1) * P], z2[:, b, :], ident)
                mm.then_inc(z2T_mm, 1)

            def logits(n, bank):
                pe.wait_ge(z2T_done, n + 1)
                for b in range(B):
                    mm = pe.matmul(bank[:, 256 + b * E:256 + (b + 1) * E], z2T[:, b, :], cen[:, :], start=True, stop=True)
                mm.then_inc(lg_mm, 1)

            def step(n, prev2, prev, cur, next1, next2):
                if cur:
                    scores(n, 0)
                    scores(n, 1)
                if prev:
                    turn_z(n - 1, (n - 1 if cur else n - 2) if prev2 else None, next1)
                if next1:
                    project_qk(n + 1, sc_done, [4 * n + i + 1 for i in range(4)])
                if not cur:
                    logits(n - 2, bankB)
                    pe.wait_ge(rank_read, n - 2)
                    project_out_pair(n - 1, 0)
                    project_out_pair(n - 1, 1)
                if cur and not next1:
                    retain(n, 0, prev)
                if prev2:
                    if next1:
                        pe.wait_ge(rot_mul, 4 * n + 5)
                        rank_tokens(n - 2, bankA)
                    elif cur:
                        pe.wait_ge(sc_done, 4 * n + 4)
                        rank_tokens(n - 2, bankC)
                    else:
                        pe.wait_ge(x2_done, n - 1)
                        rank_tokens(n - 2, bankA)
                if next1:
                    retain(n, 0, prev)
                if next1:
                    project_g(n + 1, prev2)
                if cur:
                    retain(n, 1, prev)
                    if prev2 and next1:
                        pe.wait_ge(sg_done, 4 * n + 6)
                        spread_tokens(n - 2)
                if prev and cur:
                    if next1:
                        pe.wait_ge(sg_done, 4 * n + 5)
                    else:
                        pe.wait_ge(sc_done, 4 * n + 1)
                    project_out(n - 1)
                    if not next1:
                        pe.wait_ge(sc_done, 4 * n + 2)
                        spread_tokens(n - 2)
                if not cur:
                    project_out_pair(n - 1, 2)
                    project_out_pair(n - 1, 3).then_inc(wo_mm, 1)
                if next1:
                    update_state(n, 0)
                    update_state(n, 1)
                    project_v(n + 1, prev2, prev, True)
                    if prev:
                        pe.wait_ge(z_done, 2 * n + 1)
                        turn_z2(n - 1, bankU[0][0])
                elif cur:
                    pe.wait_ge(sc_done, 4 * n + 3)
                    turn_z2(n - 1, bankB)
                else:
                    pe.wait_ge(lg_done, n - 1)
                    turn_z2(n - 1, bankB)
                    logits(n - 1, bankB)
                    pe.wait_ge(ids_add, n - 2)
                    spread_tokens(n - 2)
                if next2:
                    pe.wait_ge(z_done, 2 * n + 1)
                    x_turn(n + 2)
                if next1:
                    turn_qk(n + 1)
                if next1 and prev:
                    logits(n - 1, bankU[0][0])

            pe.wait_ge(id_in, 16)
            x_turn(0)
            pe.wait_ge(w_lo_done, 1)
            project_g(0, False)
            pe.wait_ge(w_lo_done, 2)
            project_qk(0, sg_done, [1, 2, 3, 4])
            pe.wait_ge(w_lo_done, 3)
            project_v(0, False, False, False)
            x_turn(1)
            turn_qk(0)
            step(0, False, False, True, True, True)
            pe.wait_ge(c_in[1], 16)
            pe.wait_ge(small_in, 64)
            pe.wait_ge(wo_in_sem, 16)
            step(1, False, True, True, True, True)
            with pe.Fori(2, NC - 2) as n:
                step(n, True, True, True, True, True)
            step(NC - 2, True, True, True, True, False)
            step(NC - 1, True, True, True, False, False)
            step(NC, True, True, False, False, False)

            pe.wait_ge(chosen_done, NC)
            for i, a in enumerate((before, chosen)):
                mm = pe.matmul(bankC[:, 0:E], cst[:, C_ONES], a[:, B - 1, :], start=(i == 0), stop=(i == 1))
            mm.then_inc(totals_mm, 1)
            pe.wait_ge(x2_done, NC)
            rank_tokens(NC - 1, bankA)
            pe.wait_ge(ids_add, NC - 1)
            spread_tokens(NC - 1)

            pe.wait_ge(columns_done, 1)
            pe.wait_ge(ids_add, NC)
            pe.matmul(bankC[:, 0:SLOTW], ids[:, :], slot_col[:, :], start=True, stop=True).then_inc(slots_mm, 1)

            def turn_rows(k, j, turn):
                pe.wait_ge(e_in[j], 16 * (turn + 1))
                if not (isinstance(k, int) and k < 2):
                    pe.wait_ge(exT_done, k - 1)
                pe.transpose([bankA, bankB][j % 2][:, 0:P], erow[:, j, HID:2 * HID], ident).then_inc(ezT_mm, 1)

            def first_layer(k, j):
                pe.wait_ge(w1_done, k + 1)
                pe.wait_ge(exT_done, k + 1)
                if not (isinstance(k, int) and k < 2):
                    pe.wait_ge(hid_done, k - 1)
                for c in range(FC):
                    mm = pe.matmul(bankU[0][j % 2][:, c * P:(c + 1) * P], w1_cur[:, j % 2, c * P:(c + 1) * P], exT[:, j % 2, :],
                                   start=True, stop=True)
                mm.then_inc(h_mm, 1)

            def second_layer(k, j):
                pe.wait_ge(w2_done, k + 1)
                last = isinstance(k, int) and k == SLOTS - 1
                if not last:
                    pe.wait_ge(hid_done, k + 1)
                if not (isinstance(k, int) and k < 2):
                    pe.wait_ge(eo_done, k - 1)
                for c in range(FC):
                    if last:
                        pe.wait_ge(hid_part, c + 1)
                    mm = pe.matmul(bankU[1][j % 2][:, 0:HID], hidT[:, j % 2, c, :], w2_cur[:, j, c * HID:(c + 1) * HID],
                                   start=(c == 0), stop=(c == FC - 1))
                mm.then_inc(y_mm, 1)

            def tile(k, j, turn, has_prev, has_next2):
                first_layer(k, j)
                if has_next2:
                    turn_rows(k + 2, (j + 2) % RING, turn + (j + 2) // RING)
                if has_prev:
                    second_layer(k - 1, (j - 1) % RING)

            turn_rows(0, 0, 0)
            turn_rows(1, 1, 0)
            for j in range(RING):
                tile(j, j, 0, j > 0, True)
            with pe.Fori(1, (SLOTS - 3) // RING) as m:
                for j in range(RING):
                    tile(m * RING + j, j, m, True, True)
            for j in range(3):
                tile(SLOTS - 3 + j, j, SLOTS // RING, True, j < 1)
            second_layer(SLOTS - 1, (SLOTS - 1) % RING)

        @block.vector
        def _(eng):
            chain = {"base": 0, "n": 0}

            def link(ins):
                chain["n"] += 1
                ins.then_inc(dve, 1)
                eng.wait_ge(dve, chain["base"] + chain["n"])

            def merge_stats(st, mean, tmp):
                eng.tensor_tensor(tmp[0], st[:, :, 1], st[:, :, 4], ALU.subtract)
                eng.tensor_tensor(tmp[1], st[:, :, 2], st[:, :, 5], ALU.add)
                link(eng.tensor_tensor(tmp[2], st[:, :, 1], st[:, :, 4], ALU.add))
                eng.tensor_scalar(mean, tmp[2], -0.5, None, ALU.mult)
                link(eng.tensor_tensor(tmp[0], tmp[0], tmp[0], ALU.mult))
                link(eng.scalar_tensor_tensor(out=tmp[1], in0=tmp[0], scalar=P / 4.0, in1=tmp[1], op0=ALU.mult, op1=ALU.add))

            def x_low(n):
                eng.wait_ge(xT_hi_done, n + 1)
                eng.tensor_tensor(xT_lo[:, :, :].rearrange("p b t -> p (b t)"), bankU[0][1][:, 0:B * P],
                                  xT_hi[:, :, :].rearrange("p b t -> p (b t)").bitcast(F32), ALU.subtract).then_inc(xT_lo_done, 1)

            def rotate(n, i, prev):
                eng.wait_ge(qk_mm, 4 * n + i + 1)
                src = ring[i][:, :].rearrange("p (h d) -> p h d", h=H)
                cos = cos_t[:, ds(n, 1), :].broadcast_to([P, H, D])
                if i % 2 and prev:
                    eng.wait_ge(kg_done, 2 * n - 1 + i // 2)
                eng.tensor_tensor(rot[:, i, :].rearrange("p (h d) -> p h d", h=H), src, cos, ALU.mult)
                if i >= 2:
                    eng.wait_ge(rot_add, 4 * n + i - 1)
                swapped = ring[i][:, :].rearrange("p (h s d) -> p h s d", h=H, s=2)[:, :, ::-1, :]
                sin = sin_t[:, ds(n, 1), :].rearrange("p a (s d) -> p a s d", s=2).broadcast_to([P, H, 2, D // 2])
                eng.tensor_tensor(rot_sin[:, i % 2, :].rearrange("p (h s d) -> p h s d", h=H, s=2), swapped, sin,
                                  ALU.mult).then_inc(rot_mul, 1)

            def head_stats(n, b):
                eng.wait_ge(u_mm, 2 * n + b + 1)
                for h in range(H):
                    ins = eng.bn_stats(st_u[:, b, h, :], bankU[b][h % 2][:, (h // 2) * V:(h // 2 + 1) * V])
                link(ins)
                merge_stats(st_u[:, b, :, :], mean_u[:, b, :], tmp_u)
                eng.scalar_tensor_tensor(out=ve_u[:, b, :], in0=tmp_u[1], scalar=1.0 / V, in1=cst[:, C_EPS],
                                         op0=ALU.mult, op1=ALU.add).then_inc(u_var, 1)

            def gate(n, j):
                eng.wait_ge(za_done, 4 * n + j + 1)
                y = yT[:, 2 * j:2 * j + 2, :].rearrange("p h n -> p (h n)")
                eng.tensor_tensor(y, y, sg[:, n % 2, 2 * j:2 * j + 2, :].rearrange("p h n -> p (h n)"), ALU.mult).then_inc(y_dve, 1)

            def state_add(n, b, has_prev):
                eng.wait_ge(st_mm, 2 * n + b + 1)
                bank = [bankB, bankC][b]
                if has_prev:
                    eng.wait_ge(decayed, 2 * n - 2 + b + 1)
                    ins = eng.tensor_tensor(state[:, b, :], bank[:, :], state[:, b, :], ALU.add)
                else:
                    ins = eng.tensor_copy(state[:, b, :], bank[:, :])
                ins.then_inc(st_done, 1)

            def per_token(ap, n):
                return ap.unsqueeze(2).broadcast_to([P, B, n])

            def place_tokens(n, bank):
                eng.wait_ge(rank_mm, n + 1)
                eng.tensor_tensor(placed, bank[:, 0:B * E].rearrange("p (b e) -> p b e", b=B), chosen,
                                  ALU.mult).then_inc(rank_read, 1)
                eng.wait_ge(rank_read, n + 1)
                link(eng.tensor_reduce(rank, placed, AX.X, ALU.add))
                link(eng.tensor_copy(rank_i[:, 0:2], rank))
                eng.tensor_scalar(rank_i[:, 2:4], rank_i[:, 0:2], 7, None, ALU.logical_shift_right)
                link(eng.tensor_scalar(rank_i[:, 4:6], rank_i[:, 0:2], P - 1, None, ALU.bitwise_and))
                eng.tensor_tensor(placed, chosen, per_token(cst[:, C_TOK][:, ds(n * B, B)], E), ALU.mult)
                link(eng.tensor_copy(route[:, 6:10], rank_i[:, 2:6]))
                link(eng.tensor_tensor(same_tile, cst[:, C_IOTA][:, 0:QT].unsqueeze(1).broadcast_to([P, B, QT]),
                                       per_token(tile_f, QT), ALU.is_equal))
                eng.tensor_tensor(one_row[:, :, :], cst[:, C_IOTA].unsqueeze(1).broadcast_to([P, B, P]), per_token(row_f, P), ALU.is_equal)
                eng.tensor_tensor(one_tile[:, :, :, :], placed.unsqueeze(3).broadcast_to([P, B, E, QT]),
                                  same_tile.unsqueeze(2).broadcast_to([P, B, E, QT]), ALU.mult).then_inc(one_done, 1)

            def add_tokens(n):
                eng.wait_ge(ids_mm, n + 1)
                eng.tensor_tensor(ids[:, :], ids[:, :], bankD[:, 0:P], ALU.add).then_inc(ids_add, 1)

            def choose(n):
                eng.wait_ge(lg_done, n + 1)
                link(eng.tensor_tensor(before[:, 0, :], before[:, 1, :], chosen[:, 1, :], ALU.add))
                link(eng.tensor_reduce(best, logit[:, :, :], AX.X, ALU.max))
                link(eng.tensor_tensor(eq, logit[:, :, :], per_token(best, E), ALU.is_ge))
                link(eng.tensor_tensor(eq, eq, cst[:, C_FIRST].unsqueeze(1).broadcast_to([P, B, E]), ALU.mult))
                link(eng.tensor_reduce(first, eq, AX.X, ALU.max))
                link(eng.tensor_tensor(chosen, eq, per_token(first, E), ALU.is_equal))
                eng.tensor_tensor(before[:, 1, :], before[:, 0, :], chosen[:, 0, :], ALU.add).then_inc(chosen_done, 1)
                eng.wait_ge(chosen_done, n + 1)

            def step(n, prev2, prev, cur, next1, next2):
                if cur:
                    for i in range(4):
                        eng.wait_ge(sc_mm, 4 * n + i + 1)
                        eng.tensor_tensor(prob[:, i // 2, i % 2, :], ring[i][:, :], mask_t[:, i % 2, :], ALU.mult).then_inc(sc_done, 1)
                if not cur:
                    gate(n - 1, 1)
                if prev2:
                    choose(n - 2)
                if not cur:
                    gate(n - 1, 3)
                if next1:
                    for i in range(4):
                        rotate(n + 1, i, True)
                if prev2 and (next1 or not cur):
                    place_tokens(n - 2, bankA)
                if cur:
                    head_stats(n, 0)
                    head_stats(n, 1)
                if prev2 and next1:
                    add_tokens(n - 2)
                if cur and not next1:
                    place_tokens(n - 2, bankC)
                if prev:
                    eng.wait_ge(wo_mm, n)
                    if cur:
                        eng.tensor_tensor(x2[:, :, :], x_all[:, :, ds(n - 1, 1), :].rearrange("p b a d -> p b (a d)"),
                                          bankA[:, 0:B * HID].rearrange("p (b d) -> p b d", b=B), ALU.add).then_inc(x2_done, 1)
                    else:
                        for b in range(B):
                            ins = eng.tensor_tensor(x2[:, b, :], x_all[:, b, n - 1, :], [bankC, bankU[0][0]][b][:, 0:HID], ALU.add)
                        ins.then_inc(x2_done, 1)
                    eng.wait_ge(x2_done, n)
                    for b in range(B):
                        ins = eng.bn_stats(st_z[:, b, :], x2[:, b, :])
                    link(ins)
                    merge_stats(st_z, mean_z, tmp_z)
                    eng.tensor_scalar(var_z, tmp_z[1], 1.0 / P, None, ALU.mult)
                    eng.tensor_scalar(tmp_z[2], tmp_z[1], 1.0 / P, EPS, ALU.mult, ALU.add).then_inc(z_var, 1)
                if next1:
                    state_add(n, 0, prev)
                    state_add(n, 1, prev)
                if prev:
                    eng.wait_ge(z_rstd, 2 * n - 1)
                    for b in range(B):
                        ins = eng.tensor_scalar(z2[:, b, :], x2[:, b, :], mean_z[:, b:b + 1], rs_z[:, b:b + 1], ALU.add, ALU.mult)
                    ins.then_inc(z2_done, 1)
                    eng.wait_ge(z2_done, n)
                    if prev2:
                        eng.wait_ge(pay_out, 16 * n - 16)
                    eng.wait_ge(z_rstd, 2 * n)
                    for b in range(B):
                        ins = eng.tensor_scalar(rows[:, b, HID:2 * HID], z2[:, b, :], rs2_z[:, b:b + 1], None, ALU.mult)
                    ins.then_inc(rn_done, 1)
                if cur and not next1:
                    add_tokens(n - 2)
                if next2:
                    x_low(n + 2)

            def x_stats(i, n0, n1):
                eng.wait_ge(x_in_sem[i], 16 * B)
                for n in range(n0, n1):
                    for b in range(B):
                        ins = eng.bn_stats(st_x[:, n * B + b, :], x_all[:, b, n, :])
                link(ins)
                c = slice(n0 * B, n1 * B)
                merge_stats(st_x[:, c, :], mean_x[:, c], [t[:, c] for t in tmp_x])
                eng.tensor_scalar(ve_x[:, c], tmp_x[1][:, c], 1.0 / P, EPS, ALU.mult, ALU.add).then_inc(x_var, 1)

            eng.memset(eps_x, EPS)
            eng.memset(ids[:, :], 0.0)
            eng.memset(route[:, :], 0.0)
            x_stats(0, 0, 2)
            for i in range(3):
                eng.wait_ge(w_hi_done, i + 1)
                s = slice(1024 * i, 1024 * i + 1024)
                eng.tensor_tensor(w_lo[:, s], w_raw[:, s], w_hi[:, s].bitcast(F32), ALU.subtract).then_inc(w_lo_done, 1)
                if i == 0:
                    x_low(0)
            eng.wait_ge(c_in[0], 16)
            eng.wait_ge(c_in[1], 16)
            for i in range(4):
                rotate(0, i, False)
            x_stats(1, 2, NC)
            x_low(1)
            step(0, False, False, True, True, True)
            step(1, False, True, True, True, True)
            links = 5 + 4 + 2 * 4 + 6
            base = chain["n"]
            with eng.Fori(2, NC - 2) as n:
                chain.update(base=(n - 2) * links + base, n=0)
                step(n, True, True, True, True, True)
                assert chain["n"] == links, chain["n"]
            chain.update(base=(NC - 4) * links + base, n=0)
            step(NC - 2, True, True, True, True, False)
            step(NC - 1, True, True, True, False, False)
            step(NC, True, True, False, False, False)
            choose(NC - 1)
            add_tokens(NC - 2)

            eng.wait_ge(totals_mm, 1)
            link(eng.tensor_tensor(over, bankC[:, 0:E].unsqueeze(2).broadcast_to([P, E, QT]),
                                   cst[:, C_STEP].unsqueeze(1).broadcast_to([P, E, QT]), ALU.is_gt))
            link(eng.tensor_reduce(ntile, over, AX.X, ALU.add))
            eng.tensor_scalar(spare, ntile, -1.0, float(QT), ALU.mult, ALU.add)
            link(eng.tensor_tensor_scan(tile_end, ntile, zero8, 0.0, ALU.add, ALU.add))
            place_tokens(NC - 1, bankA)
            link(eng.tensor_tensor(below, tile_end.unsqueeze(1).broadcast_to([P, SLOTW, E]),
                                   cst[:, C_SLOT].unsqueeze(2).broadcast_to([P, SLOTW, E]), ALU.is_le))
            link(eng.tensor_tensor(below2, below, spare.unsqueeze(1).broadcast_to([P, SLOTW, E]), ALU.mult))
            link(eng.tensor_reduce(col, below2, AX.X, ALU.add))
            link(eng.tensor_tensor(col, col, cst[:, C_SLOT], ALU.add))
            eng.tensor_scalar(slot_col[:, :], col, cst[:, C_PART], None, ALU.is_equal).then_inc(columns_done, 1)
            add_tokens(NC - 1)
            link(eng.tensor_reduce(passed, below, AX.X, ALU.add))
            eng.tensor_scalar(expert_i[:, :], passed[0:1, :], float(E - 1), None, ALU.min).then_inc(plan_done, 1)
            eng.wait_ge(slots_mm, 1)
            link(eng.tensor_scalar(empty, bankC[:, 0:SLOTW], 0.0, cst[:, C_PAD], ALU.is_equal, ALU.mult))
            eng.tensor_scalar(table[:, 0:SLOTW, 1], bankC[:, 0:SLOTW], -1.0, 0.0, ALU.add, ALU.max)
            eng.scalar_tensor_tensor(out=table[:, LAG:LAG + SLOTW, 0], in0=bankC[:, 0:SLOTW], scalar=-1.0, in1=empty, op0=ALU.add,
                                     op1=ALU.add).then_inc(table_done, 1)

            eng.wait_ge(b_in[1], 16)

            def take_rows(k, j, turn, e):
                eng.wait_ge(ezT_mm, k + 1)
                eng.tensor_scalar(exT[:, j % 2, :], [bankA, bankB][j % 2][:, 0:P], lng[:, ds(e, 1)], lnb[:, ds(e, 1)],
                                  ALU.mult, ALU.add).then_inc(exT_done, 1)
                if not (isinstance(k, int) and k < RING):
                    eng.wait_ge(eo_done, k - 3)
                eng.wait_ge(e_in[j], 16 * (turn + 1))
                eng.tensor_tensor(resid[:, j, :], erow[:, j, 0:HID], b2_rep[:, ds(e * HID, HID)], ALU.add).then_inc(resid_done, 1)

            def hidden(k, j, has_prev2):
                eng.wait_ge(w1_done, k + 1)
                if has_prev2:
                    eng.wait_ge(y_mm, k - 1)
                eng.wait_ge(h_mm, k + 1)
                for c in range(FC):
                    ins = eng.tensor_scalar(hidT[:, j % 2, c, :], bankU[0][j % 2][:, c * P:(c + 1) * P], b1_cur[:, j, c:c + 1], 0.0,
                                            ALU.add, ALU.max)
                    if isinstance(k, int) and k == SLOTS - 1:
                        ins.then_inc(hid_part, 1)
                if not (isinstance(k, int) and k == SLOTS - 1):
                    ins.then_inc(hid_done, 1)

            def finish(k, j):
                eng.wait_ge(y_mm, k + 1)
                eng.wait_ge(resid_done, k + 1)
                eng.tensor_tensor(eout[:, j, :], bankU[1][j % 2][:, 0:HID], resid[:, j, :], ALU.add).then_inc(eo_done, 1)

            def expert(k):
                return eng.value_load(expert_i[0:1, ds(k, 1)], min_val=0, max_val=E - 1)

            def tile(k, j, turn, has_prev, has_next2, stored=None):
                e = expert(k + 2) if has_next2 else None
                hidden(k, j, stored is not None or j >= 2)
                if has_next2:
                    take_rows(k + 2, (j + 2) % RING, turn + (j + 2) // RING, e)
                if stored is not None and j > 0:
                    eng.wait_ge(e_out[j - 1], stored)
                if stored is not None and j == RING - 1:
                    eng.wait_ge(e_out[j], stored)
                if has_prev:
                    finish(k - 1, (j - 1) % RING)

            eng.wait_ge(plan_done, 1)
            for j in range(2):
                take_rows(j, j, 0, expert(j))
            for j in range(RING):
                tile(j, j, 0, j > 0, True)
            with eng.Fori(1, (SLOTS - 3) // RING) as m:
                for j in range(RING):
                    tile(m * RING + j, j, m, True, True, 16 * m)
            for j in range(3):
                tile(SLOTS - 3 + j, j, SLOTS // RING, True, j < 1, 16 * (SLOTS // RING))
            eng.wait_ge(e_out[2], 16 * (SLOTS // RING))
            finish(SLOTS - 1, (SLOTS - 1) % RING)


def kernel(L0_attn_x, L0_attn_Wq, L0_attn_Wk, L0_attn_Wv, L0_attn_Wg, L0_attn_Wo, L0_attn_gn_weight, L0_attn_gn_bias,
           L0_ffn_centroids, L0_ffn_ln_g, L0_ffn_ln_b, L0_ffn_W1, L0_ffn_b1, L0_ffn_W2, L0_ffn_b2):
    import concourse.bacc as bacc
    from concourse.bass_utils import run_bass_kernel_spmd

    def a(v):
        return np.asarray(v)

    c = np.ascontiguousarray
    ins = {
        "x": c(a(L0_attn_x)),
        "wqkvg": c(np.concatenate([a(w) for w in (L0_attn_Wg, L0_attn_Wq, L0_attn_Wk, L0_attn_Wv)], 0).T),
        "wo": c(a(L0_attn_Wo).reshape(HID, H, V).transpose(2, 1, 0)),
        "gn": c(np.stack([a(L0_attn_gn_weight), a(L0_attn_gn_bias)]).reshape(2, H, V).transpose(2, 0, 1)),
        "cen": c(a(L0_ffn_centroids).T),
        "lng": c(a(L0_ffn_ln_g).T),
        "lnb": c(a(L0_ffn_ln_b).T),
        "w1": c(a(L0_ffn_W1).transpose(1, 0, 2).reshape(HID, E * F)),
        "b1": c(a(L0_ffn_b1).reshape(E, FC, P).transpose(2, 0, 1).reshape(P, E * FC)),
        "w2": c(a(L0_ffn_W2).reshape(E, FC, P, HID).transpose(2, 0, 1, 3)),
        "b2": c(a(L0_ffn_b2).reshape(-1)),
        "constants": constants(),
    }
    nc = bacc.Bacc("TRN2", target_bir_lowering=False, num_devices=1)
    args = [nc.dram_tensor(f"in_{n}", v.shape, mybir.dt.from_np(v.dtype), kind="ExternalInput").ap() for n, v in ins.items()]
    out = nc.dram_tensor("out", (B, T, HID), F32, kind="ExternalOutput").ap()
    preln_retention_moe_kernel(nc, *args, out)
    r = run_bass_kernel_spmd(nc, [{f"in_{n}": v for n, v in ins.items()}], core_ids=[0])
    return r.results[0]["out"]
```
